# Optimizing a Trainium2 kernel written in Bass

```python
import numpy as np
import jax
import jax.numpy as jnp

def _softmax(x, axis=-1):
    return jax.nn.softmax(x, axis=axis)

def _gelu(x):
    return jax.nn.gelu(x, approximate=True)

def _silu(x):
    return jax.nn.silu(x)

def _sigmoid(x):
    return jax.nn.sigmoid(x)

def _layernorm(x, axis=-1, eps=1e-05):
    m = jnp.mean(x, axis=axis, keepdims=True)
    v = jnp.var(x, axis=axis, keepdims=True)
    return (x - m) / jnp.sqrt(v + eps)

def _scatter_add(tgt, idx, src, axis=0):
    return tgt.at[idx].add(src)

def _segment_sum(src, seg, n):
    return jax.ops.segment_sum(src, seg, n)
kernel_name = 'mk_seq_preln_d1_jaxref_r4_b75da5'

def setup_inputs(seed: int=0):
    np.random.seed(seed)
    _w = jnp.asarray

    def _L0_attn_setup():
        import jax, jax.numpy as jnp
        import numpy as np
        import math
        D_MODEL = 256
        NUM_HEADS = 16
        B, L = (2, 512)
        PERIODS = (1.0, 30.0)
        WEIGHTS = (0.8, 0.4)
        SIGMAS = (0.5, 2.0)

        def _gaussian_mask(length):
            idx = jnp.arange(length, dtype=jnp.float32)
            delta = jnp.abs(idx[:, None] - idx[None, :])
            mask = jnp.zeros_like(delta)
            for p, w, sigma in zip(PERIODS, WEIGHTS, SIGMAS):
                if p < 0.2:
                    continue
                mask = mask + w * jnp.exp(-(delta - p) ** 2 / (2.0 * sigma ** 2))
            return mask
        key = jax.random.key(seed)
        ks = jax.random.split(key, 10)
        s = 1.0 / math.sqrt(D_MODEL)
        inp = {'x': jax.random.normal(ks[0], (B, L, D_MODEL), dtype=jnp.float32), 'Wq': jax.random.normal(ks[1], (D_MODEL, D_MODEL), dtype=jnp.float32) * s, 'bq': jax.random.normal(ks[2], (D_MODEL,), dtype=jnp.float32) * 0.01, 'Wk': jax.random.normal(ks[3], (D_MODEL, D_MODEL), dtype=jnp.float32) * s, 'bk': jax.random.normal(ks[4], (D_MODEL,), dtype=jnp.float32) * 0.01, 'Wv': jax.random.normal(ks[5], (D_MODEL, D_MODEL), dtype=jnp.float32) * s, 'bv': jax.random.normal(ks[6], (D_MODEL,), dtype=jnp.float32) * 0.01, 'Wo': jax.random.normal(ks[7], (D_MODEL, D_MODEL), dtype=jnp.float32) * s, 'bo': jax.random.normal(ks[8], (D_MODEL,), dtype=jnp.float32) * 0.01, 'prior_lambda': jnp.asarray(2.0, dtype=jnp.float32)}
        return inp
    _L0_attn_in = _L0_attn_setup()

    def _L0_ffn_setup():
        import jax, jax.numpy as jnp
        import numpy as np
        DIM = 256
        DEPTH = 2
        HEADS = 8
        DIM_HEAD = 64
        WINDOW = 128
        INNER = HEADS * DIM_HEAD
        HID = int(DIM * 4 * 2 / 3)
        B, N = (2, 2048)
        QK_SCALE = 8.0

        def shift_token(t):
            t1, t2 = jnp.split(t, 2, axis=-1)
            t2 = jnp.pad(t2, ((0, 0), (1, 0), (0, 0)))[:, :-1]
            return jnp.concatenate([t1, t2], axis=-1)

        def l2norm(t):
            return t / jnp.clip(jnp.linalg.norm(t, axis=-1, keepdims=True), 1e-12)

        def rotate_half(x):
            x1, x2 = jnp.split(x, 2, axis=-1)
            return jnp.concatenate([-x2, x1], axis=-1)

        def rotary_xpos(q, k):
            n = q.shape[-2]
            half_idx = jnp.arange(0, DIM_HEAD, 2, dtype=jnp.float32)
            inv_freq = 1.0 / 10000.0 ** (half_idx / DIM_HEAD)
            t = jnp.arange(n, dtype=jnp.float32)
            freqs = t[:, None] * inv_freq[None, :]
            freqs = jnp.concatenate([freqs, freqs], axis=-1)
            base = (half_idx + 0.4 * DIM_HEAD) / (1.4 * DIM_HEAD)
            power = (t - n // 2) / float(WINDOW // 2)
            scale = base[None, :] ** power[:, None]
            scale = jnp.concatenate([scale, scale], axis=-1)
            cos, sin = (jnp.cos(freqs), jnp.sin(freqs))
            q = q * cos * scale + rotate_half(q) * sin * scale
            k = k * cos / scale + rotate_half(k) * sin / scale
            return (q, k)

        def local_attention(q, k, v):
            b, h, n, d = q.shape
            w = n // WINDOW
            bq = q.reshape(b, h, w, WINDOW, d) * QK_SCALE
            bk = k.reshape(b, h, w, WINDOW, d)
            bv = v.reshape(b, h, w, WINDOW, d)

            def look_around(t):
                p = jnp.pad(t, ((0, 0), (0, 0), (1, 0), (0, 0), (0, 0)))
                return jnp.concatenate([p[:, :, :w], p[:, :, 1:]], axis=3)
            bk, bv = (look_around(bk), look_around(bv))
            bt = jnp.arange(n).reshape(w, WINDOW)
            btp = jnp.pad(bt, ((1, 0), (0, 0)), constant_values=-1)
            btk = jnp.concatenate([btp[:w], btp[1:]], axis=1)
            sim = jnp.einsum('bhwid,bhwjd->bhwij', bq, bk)
            i = bt[:, :, None]
            j = btk[:, None, :]
            mask = (i < j) | (i > j + WINDOW) | (j == -1)
            sim = jnp.where(mask, -jnp.finfo(sim.dtype).max, sim)
            attn = jax.nn.softmax(sim, axis=-1)
            out = jnp.einsum('bhwij,bhwjd->bhwid', attn, bv)
            return out.reshape(b, h, n, d)

        def _layer(x, wqkv, qs, ksc, wo, lg, lb, w1, b1, w2, b2):
            b, n, _ = x.shape
            h = shift_token(x)
            qkv = h @ wqkv
            q, k, v = jnp.split(qkv, 3, axis=-1)
            to_heads = lambda t: t.reshape(b, n, HEADS, DIM_HEAD).transpose(0, 2, 1, 3)
            q, k, v = (to_heads(q), to_heads(k), to_heads(v))
            q = l2norm(q) * qs
            k = l2norm(k) * ksc
            q, k = rotary_xpos(q, k)
            o = local_attention(q, k, v)
            o = o.transpose(0, 2, 1, 3).reshape(b, n, INNER)
            x = x + o @ wo
            h = shift_token(x)
            mu = h.mean(-1, keepdims=True)
            var = h.var(-1, keepdims=True)
            h = (h - mu) / jnp.sqrt(var + 1e-05) * lg + lb
            h = h @ w1 + b1
            a, g = jnp.split(h, 2, axis=-1)
            h = a * jax.nn.gelu(g, approximate=False)
            x = x + h @ w2 + b2
            return x
        key = jax.random.key(seed)
        ks = jax.random.split(key, 6)
        return {'x': jax.random.normal(ks[0], (B, N, DIM), jnp.float32), 'wqkv': jax.random.normal(ks[1], (DEPTH, DIM, 3 * INNER), jnp.float32) * 0.02, 'q_scale': jnp.ones((DEPTH, DIM_HEAD), jnp.float32), 'k_scale': jnp.ones((DEPTH, DIM_HEAD), jnp.float32), 'wo': jax.random.normal(ks[2], (DEPTH, INNER, DIM), jnp.float32) * 0.02, 'ln_g': jnp.ones((DEPTH, DIM), jnp.float32), 'ln_b': jnp.zeros((DEPTH, DIM), jnp.float32), 'w1': jax.random.normal(ks[3], (DEPTH, DIM, 2 * HID), jnp.float32) * 0.02, 'b1': jnp.zeros((DEPTH, 2 * HID), jnp.float32), 'w2': jax.random.normal(ks[4], (DEPTH, HID, DIM), jnp.float32) * 0.02, 'b2': jnp.zeros((DEPTH, DIM), jnp.float32)}
    _L0_ffn_in = _L0_ffn_setup()
    _d = {'L0_attn_x': _L0_attn_in['x'], 'L0_attn_Wq': _L0_attn_in['Wq'], 'L0_attn_bq': _L0_attn_in['bq'], 'L0_attn_Wk': _L0_attn_in['Wk'], 'L0_attn_bk': _L0_attn_in['bk'], 'L0_attn_Wv': _L0_attn_in['Wv'], 'L0_attn_bv': _L0_attn_in['bv'], 'L0_attn_Wo': _L0_attn_in['Wo'], 'L0_attn_bo': _L0_attn_in['bo'], 'L0_attn_prior_lambda': _L0_attn_in['prior_lambda'], 'L0_ffn_wqkv': _L0_ffn_in['wqkv'], 'L0_ffn_q_scale': _L0_ffn_in['q_scale'], 'L0_ffn_k_scale': _L0_ffn_in['k_scale'], 'L0_ffn_wo': _L0_ffn_in['wo'], 'L0_ffn_ln_g': _L0_ffn_in['ln_g'], 'L0_ffn_ln_b': _L0_ffn_in['ln_b'], 'L0_ffn_w1': _L0_ffn_in['w1'], 'L0_ffn_b1': _L0_ffn_in['b1'], 'L0_ffn_w2': _L0_ffn_in['w2'], 'L0_ffn_b2': _L0_ffn_in['b2']}
    _x0 = _d['L0_attn_x']
    _d['L0_attn_x'] = jax.random.normal(jax.random.fold_in(jax.random.key(seed), 1), (4, 2048, 256), dtype=_x0.dtype)
    del _x0
    return _d

def reference(L0_attn_x, L0_attn_Wq, L0_attn_bq, L0_attn_Wk, L0_attn_bk, L0_attn_Wv, L0_attn_bv, L0_attn_Wo, L0_attn_bo, L0_attn_prior_lambda, L0_ffn_wqkv, L0_ffn_q_scale, L0_ffn_k_scale, L0_ffn_wo, L0_ffn_ln_g, L0_ffn_ln_b, L0_ffn_w1, L0_ffn_b1, L0_ffn_w2, L0_ffn_b2):

    def _L0_attn_ref(x, Wq, bq, Wk, bk, Wv, bv, Wo, bo, prior_lambda):
        import jax, jax.numpy as jnp
        import numpy as np
        import math
        D_MODEL = 256
        NUM_HEADS = 16
        B, L = (2, 512)
        PERIODS = (1.0, 30.0)
        WEIGHTS = (0.8, 0.4)
        SIGMAS = (0.5, 2.0)

        def _gaussian_mask(length):
            idx = jnp.arange(length, dtype=jnp.float32)
            delta = jnp.abs(idx[:, None] - idx[None, :])
            mask = jnp.zeros_like(delta)
            for p, w, sigma in zip(PERIODS, WEIGHTS, SIGMAS):
                if p < 0.2:
                    continue
                mask = mask + w * jnp.exp(-(delta - p) ** 2 / (2.0 * sigma ** 2))
            return mask
        Bx, Lx, D = x.shape
        H = NUM_HEADS
        hd = D // H

        def split_heads(t):
            return t.reshape(Bx, Lx, H, hd).transpose(0, 2, 1, 3)
        Q = split_heads(x @ Wq.T + bq)
        K = split_heads(x @ Wk.T + bk)
        V = split_heads(x @ Wv.T + bv)
        scores = jnp.einsum('bhqd,bhkd->bhqk', Q, K) / math.sqrt(hd)
        scores = scores + prior_lambda * _gaussian_mask(Lx)[None, None, :, :]
        attn = jax.nn.softmax(scores, axis=-1)
        out = jnp.einsum('bhqk,bhkd->bhqd', attn, V)
        out = out.transpose(0, 2, 1, 3).reshape(Bx, Lx, D)
        return out @ Wo.T + bo

    def _L0_ffn_ref(x, wqkv, q_scale, k_scale, wo, ln_g, ln_b, w1, b1, w2, b2):
        import jax, jax.numpy as jnp
        import numpy as np
        DIM = 256
        DEPTH = 2
        HEADS = 8
        DIM_HEAD = 64
        WINDOW = 128
        INNER = HEADS * DIM_HEAD
        HID = int(DIM * 4 * 2 / 3)
        B, N = (2, 2048)
        QK_SCALE = 8.0

        def shift_token(t):
            t1, t2 = jnp.split(t, 2, axis=-1)
            t2 = jnp.pad(t2, ((0, 0), (1, 0), (0, 0)))[:, :-1]
            return jnp.concatenate([t1, t2], axis=-1)

        def l2norm(t):
            return t / jnp.clip(jnp.linalg.norm(t, axis=-1, keepdims=True), 1e-12)

        def rotate_half(x):
            x1, x2 = jnp.split(x, 2, axis=-1)
            return jnp.concatenate([-x2, x1], axis=-1)

        def rotary_xpos(q, k):
            n = q.shape[-2]
            half_idx = jnp.arange(0, DIM_HEAD, 2, dtype=jnp.float32)
            inv_freq = 1.0 / 10000.0 ** (half_idx / DIM_HEAD)
            t = jnp.arange(n, dtype=jnp.float32)
            freqs = t[:, None] * inv_freq[None, :]
            freqs = jnp.concatenate([freqs, freqs], axis=-1)
            base = (half_idx + 0.4 * DIM_HEAD) / (1.4 * DIM_HEAD)
            power = (t - n // 2) / float(WINDOW // 2)
            scale = base[None, :] ** power[:, None]
            scale = jnp.concatenate([scale, scale], axis=-1)
            cos, sin = (jnp.cos(freqs), jnp.sin(freqs))
            q = q * cos * scale + rotate_half(q) * sin * scale
            k = k * cos / scale + rotate_half(k) * sin / scale
            return (q, k)

        def local_attention(q, k, v):
            b, h, n, d = q.shape
            w = n // WINDOW
            bq = q.reshape(b, h, w, WINDOW, d) * QK_SCALE
            bk = k.reshape(b, h, w, WINDOW, d)
            bv = v.reshape(b, h, w, WINDOW, d)

            def look_around(t):
                p = jnp.pad(t, ((0, 0), (0, 0), (1, 0), (0, 0), (0, 0)))
                return jnp.concatenate([p[:, :, :w], p[:, :, 1:]], axis=3)
            bk, bv = (look_around(bk), look_around(bv))
            bt = jnp.arange(n).reshape(w, WINDOW)
            btp = jnp.pad(bt, ((1, 0), (0, 0)), constant_values=-1)
            btk = jnp.concatenate([btp[:w], btp[1:]], axis=1)
            sim = jnp.einsum('bhwid,bhwjd->bhwij', bq, bk)
            i = bt[:, :, None]
            j = btk[:, None, :]
            mask = (i < j) | (i > j + WINDOW) | (j == -1)
            sim = jnp.where(mask, -jnp.finfo(sim.dtype).max, sim)
            attn = jax.nn.softmax(sim, axis=-1)
            out = jnp.einsum('bhwij,bhwjd->bhwid', attn, bv)
            return out.reshape(b, h, n, d)

        def _layer(x, wqkv, qs, ksc, wo, lg, lb, w1, b1, w2, b2):
            b, n, _ = x.shape
            h = shift_token(x)
            qkv = h @ wqkv
            q, k, v = jnp.split(qkv, 3, axis=-1)
            to_heads = lambda t: t.reshape(b, n, HEADS, DIM_HEAD).transpose(0, 2, 1, 3)
            q, k, v = (to_heads(q), to_heads(k), to_heads(v))
            q = l2norm(q) * qs
            k = l2norm(k) * ksc
            q, k = rotary_xpos(q, k)
            o = local_attention(q, k, v)
            o = o.transpose(0, 2, 1, 3).reshape(b, n, INNER)
            x = x + o @ wo
            h = shift_token(x)
            mu = h.mean(-1, keepdims=True)
            var = h.var(-1, keepdims=True)
            h = (h - mu) / jnp.sqrt(var + 1e-05) * lg + lb
            h = h @ w1 + b1
            a, g = jnp.split(h, 2, axis=-1)
            h = a * jax.nn.gelu(g, approximate=False)
            x = x + h @ w2 + b2
            return x
        for l in range(DEPTH):
            x = _layer(x, wqkv[l], q_scale[l], k_scale[l], wo[l], ln_g[l], ln_b[l], w1[l], b1[l], w2[l], b2[l])
        return x
    x = L0_attn_x
    x = x + _L0_attn_ref(_layernorm(x, axis=-1), L0_attn_Wq, L0_attn_bq, L0_attn_Wk, L0_attn_bk, L0_attn_Wv, L0_attn_bv, L0_attn_Wo, L0_attn_bo, L0_attn_prior_lambda)
    x = x + _L0_ffn_ref(_layernorm(x, axis=-1), L0_ffn_wqkv, L0_ffn_q_scale, L0_ffn_k_scale, L0_ffn_wo, L0_ffn_ln_g, L0_ffn_ln_b, L0_ffn_w1, L0_ffn_b1, L0_ffn_w2, L0_ffn_b2)
    return x

_drawn_inputs = setup_inputs


def setup_inputs(seed=0):
    import zlib

    import numpy as np

    out = dict(_drawn_inputs(seed))
    spreads = {'L0_ffn_q_scale': (1.0, 0.6),
     'L0_ffn_k_scale': (1.0, 0.6),
     'L0_ffn_ln_g': (1.0, 0.6),
     'L0_ffn_ln_b': (0.0, 0.8),
     'L0_ffn_b1': (0.0, 0.8),
     'L0_ffn_b2': (0.0, 0.1)}
    factors = {'L0_attn_bq': 34.902,
     'L0_attn_bk': 64.0,
     'L0_attn_bv': 5.647,
     'L0_attn_bo': 5.856,
     'L0_ffn_wqkv': 3.492,
     'L0_ffn_wo': 3.423}
    for name, (base, spread) in spreads.items():
        noise = np.random.default_rng([zlib.crc32(name.encode()), seed]).standard_normal(out[name].shape)
        drawn = base * np.exp(spread * noise) if base else spread * noise
        out[name] = jnp.asarray(drawn.astype(out[name].dtype))
    for name, factor in factors.items():
        out[name] = (out[name] * factor).astype(out[name].dtype)
    return out
```

```python
from contextlib import ExitStack

import numpy as np
import concourse.bass as bass
from concourse import mybir

F32 = mybir.dt.float32
BF16 = mybir.dt.bfloat16
ALU = mybir.AluOpType
ACT = mybir.ActivationFunctionType
X = mybir.AxisListType.X

NB, L, D = 4, 2048, 256
W = L // 128
NT = NB * W
EPS = 1e-5
HA, DA = 16, 16
BAND = 59
WIN = 32 + 2 * BAND
QPART = [0, 1, 2, 0, 1, 0]
KPART = [0, 0, 0, 1, 1, 2]


class Op:
    def __init__(self, lane, fn, waits, sem=None, val=None):
        self.lane, self.fn, self.waits = lane, fn, waits
        self.sem, self.val, self.signals, self.dma = sem, val, False, sem is not None


def flat(waits):
    out = []
    for w in waits:
        out += flat(w) if isinstance(w, (list, tuple)) else [] if w is None else [w]
    return out


class Lane:

    def __init__(self, sem):
        self.sem, self.ops = sem, []

    def __call__(self, fn, *waits):
        op = Op(self, fn, flat(waits))
        for w in op.waits:
            w.signals = True
        self.ops.append(op)
        return op

    def dma(self, counter, fn, *waits):
        counter.n += 16
        op = Op(self, fn, flat(waits), counter.sem, counter.n)
        for w in op.waits:
            w.signals = True
        self.ops.append(op)
        return op

    def number(self):
        n = 0
        for op in self.ops:
            if op.signals and not op.dma:
                n += 1
                op.sem, op.val = self.sem, n

    def emit(self, eng):
        seen = {}
        for op in self.ops:
            need = {}
            for w in op.waits:
                need[w.sem] = max(need.get(w.sem, 0), w.val)
            for s, v in need.items():
                if seen.get(s, 0) < v:
                    eng.wait_ge(s, v)
                    seen[s] = v
            inst = op.fn and op.fn(eng)
            if op.dma:
                inst.then_inc(op.sem, 16)
            elif op.signals:
                inst.then_inc(op.sem, 1)


class Counter:

    def __init__(self, sem):
        self.sem, self.n = sem, 0


class Phase:

    def __init__(self, nc, tag):
        self.nc, self.tag, self.ctx = nc, tag, ExitStack()
        self.pe, self.act, self.dve, self.pool, self.sp = (Lane(self.sem(n)) for n in ("pe", "act", "dve", "pool", "sp"))

    def sem(self, name):
        return self.ctx.enter_context(self.nc.semaphore(f"{self.tag}_{name}"))

    def counter(self, name):
        return Counter(self.sem(name))

    def sb(self, name, shape, dt=F32):
        return self.ctx.enter_context(self.nc.sbuf_tensor(f"{self.tag}_{name}", shape, dt))

    def ps(self, name, shape, dt=F32):
        return self.ctx.enter_context(self.nc.psum_tensor(f"{self.tag}_{name}", shape, dt))

    def run(self):
        lanes = dict(tensor=self.pe, scalar=self.act, vector=self.dve, gpsimd=self.pool, sync=self.sp)
        for lane in lanes.values():
            lane.number()
        with self.nc.Block() as block:
            for name, lane in lanes.items():
                def body(eng, lane=lane):
                    lane.emit(eng)
                {"tensor": block.tensor, "scalar": block.scalar, "vector": block.vector,
                 "gpsimd": block.gpsimd, "sync": block.sync}[name](body)
        self.ctx.close()


def prior():
    i, c = np.arange(32, dtype=np.float32)[:, None], np.arange(WIN, dtype=np.float32)[None, :]
    delta = np.abs(c - np.float32(BAND) - i)
    g = np.zeros_like(delta)
    for p, w, s in ((1.0, 0.8, 0.5), (30.0, 0.4, 2.0)):
        g = g + np.float32(w) * np.exp(-(delta - np.float32(p)) ** 2 / np.float32(2.0 * s * s))
    g[delta > BAND] = 0.0
    return np.concatenate([g, g, g]).astype(np.float32)


def windows(r0):
    a, e = max(r0 - BAND, 0), min(r0 - BAND + WIN, L)
    while a < e:
        z = min(e, (a // 512 + 1) * 512)
        yield a // 512, a % 512, a - (r0 - BAND), z - a
        a = z


def attention(nc, xs, x1, a):
    ph = Phase(nc, "a")
    pe, act, dve, pool, sp = ph.pe, ph.act, ph.dve, ph.pool, ph.sp
    sb = ph.sb
    hT = sb("hT", [128, 2, L])
    at = hT[:, :, :].rearrange("p c (w d) -> p (c w) d", d=D)
    parts = {"q": sb("qs", [128, 2, 3, L], BF16), "k": sb("ks", [128, 2, 3, L], BF16)}
    qp = [sb(f"qp{i}", [128, L], BF16) for i in range(3)]
    kp = [sb(f"kp{i}", [128, L], BF16) for i in range(3)]
    v = sb("v", [128, W, HA, DA + 1])
    NP = 5
    pr = [sb(f"pr{i}", [128, 1024]) for i in range(NP)]
    wt = {n: sb("w" + n, [128, 2, D]) for n in "qkvo"}
    bias = {n: sb("b" + n, [128, 2]) for n in "qk"}
    brow = {n: sb("r" + n, [128, D]) for n in "vo"}
    ident = sb("ident", [128, 128])
    identb = sb("identb", [128, 128], BF16)
    gt = sb("gt", [96, WIN])
    g1, g2 = sb("g1", [96, WIN]), sb("g2", [96, WIN])
    gp = [sb(f"gp{i}", [96, WIN], BF16) for i in range(3)]
    mt = sb("mt", [96, WIN], BF16)
    sel = sb("sel", [96, 32], BF16)
    self32 = sb("self32", [96, 32])
    lam, lam4 = sb("lam", [128, 1]), sb("lam4", [128, 1])
    nh = sb("nh", [128, W])
    st = sb("st", [128, W, 6])
    mv = sb("mv", [128, W, 2])
    ve, rs = sb("ve", [128, W]), sb("rs", [128, W])
    hn = [pr[2][:, 0:256], pr[2][:, 256:512]]
    tmp = [pr[3][:, 0:512], pr[4][:, 0:512]]
    mx = [sb(f"mx{i}", [128, W, 4]) for i in range(2)]
    nm, r1 = sb("nm", [128, W]), sb("r1", [128, W])
    pk = sb("pk", [128, 3, W], BF16)
    row = sb("row", [48, 128], BF16)
    osb = sb("osb", [128, 512])
    rc = sb("rc", [128, 4, 4])
    bank = [ph.ps(f"b{i}", [128, 512]) for i in range(2)]
    wide = [ph.ps(f"w{i}", [128, 1024]) for i in range(2)]
    po = ph.ps("po", [128, 512])
    pt = ph.ps("pt", [128, 512])

    cw = ph.counter("cw")
    for n in "qkvo":
        sp.dma(cw, lambda e, n=n: e.dma_start(wt[n][:, :, :], a["w" + n].rearrange("(c p) n -> p c n", p=128)))
    for n in "qk":
        sp.dma(cw, lambda e, n=n: e.dma_start(bias[n][:, :], a["b" + n]))
    for n in "vo":
        sp.dma(cw, lambda e, n=n: e.dma_start(brow[n][:, :], a["b" + n].partition_broadcast(128)))
    sp.dma(cw, lambda e: e.dma_start(lam[:, :], a["lam"].partition_broadcast(128)))
    sp.dma(cw, lambda e: e.dma_start(gt[:, :], a["prior"]))
    sp.dma(cw, lambda e: e.dma_start(self32[:, :], a["sel"]))
    const = sp.dma(cw, lambda e: e.dma_start(ident[:, :], a["ident"]))
    cx = [ph.counter(f"x{b}") for b in range(NB)]
    xin = [sp.dma(cx[b], lambda e, b=b: e.dma_start(xs[:, b * W:(b + 1) * W, :], a["x"][b].rearrange("(w p) d -> p w d", p=128)))
           for b in range(NB)]

    idb = dve(lambda e: e.tensor_copy(identb[:, :], ident[:, :]), const)
    c_sel = dve(lambda e: e.tensor_copy(sel[:, :], self32[:, :]), const)
    c_nh = dve(lambda e: e.memset(nh[:, :], -0.5))
    t = dve(lambda e: e.tensor_scalar(lam4[:, :], lam[:, :], 4.0, None, ALU.mult), const)
    t = dve(lambda e: e.tensor_scalar(gt[:, :], gt[:, :], lam4[0:96, :], None, ALU.mult), t)
    t = dve(lambda e: e.tensor_copy(gp[0][:, :], gt[:, :]), t)
    t = dve(lambda e: e.tensor_tensor(g1[:, :], gt[:, :], gp[0][:, :], ALU.subtract), t)
    t = dve(lambda e: e.tensor_copy(gp[1][:, :], g1[:, :]), t)
    t = dve(lambda e: e.tensor_tensor(g2[:, :], g1[:, :], gp[1][:, :], ALU.subtract), t)
    t = dve(lambda e: e.tensor_copy(gp[2][:, :], g2[:, :]), t)
    for i in range(3):
        c_mt = dve(lambda e, i=i: e.tensor_copy(mt[32 * i:32 * i + 32, :], gp[i][32 * i:32 * i + 32, :]), t)
    for i in range(3):
        c_one = dve(lambda e, i=i: e.memset(kp[i][96:99, :], 1.0))
    c_v1 = dve(lambda e: e.memset(v[:, :, :, DA:DA + 1], 1.0))
    c_po = dve(lambda e: e.memset(po[:, :], 0.0))

    pools = bank + [wide[0][:, 0:512], wide[0][:, 512:1024], wide[1][:, 0:512], wide[1][:, 512:1024]]
    freed = [None] * 6
    turn = [0]

    def slot():
        i = turn[0] % 6
        turn[0] += 1
        return i, pools[i][:, :] if i < 2 else pools[i]

    cp = [ph.counter(f"pack{i}") for i in range(3)]
    cr = [ph.counter(f"row{i}") for i in range(3)]
    cs = ph.counter("res")
    pack_of, row_of, qk_read = {}, {}, {}
    free_bank, free_wide = [None] * 2, [None] * 2
    free_pr, free_pt, free_hn, free_tmp = [None] * NP, None, [None] * 2, [None] * 2
    free_mx = [None] * 2
    free_po, free_osb, free_row, free_pk = c_po, None, None, None
    pv_last, norm_last = None, None
    final_reads = None
    pack_last = None
    x1_done = None

    for b in range(NB):
        free_hn, free_tmp = [free_pr[2]] * 2, free_pr[3:5]
        for w in range(W):
            t = dve(lambda e, w=w, b=b: e.bn_stats(st[:, w, :], xs[:, b * W + w, :]), xin[b])
            t = dve(lambda e, w=w: e.bn_aggr(mv[:, w, :], st[:, w, :]), t)
        t = dve(lambda e: e.tensor_scalar(ve[:, :], mv[:, :, 1], EPS, None, ALU.add), t)
        t_rs = pool(lambda e: e.tensor_tensor(rs[:, :], ve[:, :], nh[:, :], ALU.pow), t, c_nh)
        tevac = []
        for w0 in range(0, W, 2):
            i, bk = slot()
            tr = None
            for w in (w0, w0 + 1):
                n = dve(lambda e, w=w, b=b: e.tensor_scalar(hn[w % 2], xs[:, b * W + w, :], mv[:, w, 0:1], rs[:, w:w + 1],
                                                           ALU.subtract, ALU.mult), t_rs, free_hn[w % 2])
                for c in range(2):
                    tr = pe(lambda e, w=w, c=c, bk=bk: e.transpose(bk[:, c * 256 + (w % 2) * 128:c * 256 + (w % 2) * 128 + 128],
                                                                   hn[w % 2][:, c * 128:c * 128 + 128], ident[:, :]), n, freed[i])
                free_hn[w % 2] = tr
            tevac.append(act(lambda e, w0=w0, bk=bk: e.activation(
                hT[:, :, w0 * 128:w0 * 128 + 256], bk.rearrange("p (c n) -> p c n", c=2), ACT.Copy), tr, final_reads))
            freed[i] = tevac[-1]
        split = []
        k = 0
        for c in range(2):
            for j in range(4):
                for n in "qk":
                    i, bk = slot()
                    for cc in range(2):
                        m = pe(lambda e, n=n, c=c, cc=cc, j=j, bk=bk: e.matmul(
                            bk, wt[n][:, cc, c * 128:c * 128 + 128], hT[:, cc, j * 512:j * 512 + 512],
                            start=cc == 0, stop=cc == 1), tevac[2 * j + 1], freed[i])
                    dst = [parts[n][:, c, p, j * 512:j * 512 + 512] for p in range(3)]
                    tm = tmp[k % 2]
                    h0 = act(lambda e, bk=bk, d=dst[0], n=n, c=c: e.activation(d, bk, ACT.Identity, bias=bias[n][:, c:c + 1]), m, pack_last)
                    r = dve(lambda e, bk=bk, d=dst[0], n=n, c=c, tm=tm: e.scalar_tensor_tensor(
                        tm, bk, bias[n][:, c:c + 1], d, ALU.add, ALU.subtract), h0, free_tmp[k % 2])
                    freed[i] = r
                    h1 = act(lambda e, d=dst[1], tm=tm: e.activation(d, tm, ACT.Copy), r)
                    h2 = pool(lambda e, d=dst[2], d1=dst[1], tm=tm: e.tensor_tensor(d, tm, d1, ALU.subtract), h1, pack_last)
                    free_tmp[k % 2] = h2
                    split.append(h2)
                    k += 1
        vdone = None
        for w in range(W):
            i, bk = slot()
            for cc in range(2):
                m = pe(lambda e, cc=cc, w=w, bk=bk: e.matmul(bk[:, 0:D], hT[:, cc, w * 128:w * 128 + 128], wt["v"][:, cc, :],
                                                            start=cc == 0, stop=cc == 1), tevac[w // 2], freed[i])
            vdone = dve(lambda e, w=w, bk=bk: e.tensor_tensor(
                v[:, w, :, 0:DA], bk[:, 0:D].rearrange("p (h d) -> p h d", d=DA),
                brow["v"][:, :].rearrange("p (h d) -> p h d", d=DA), ALU.add), m, pv_last)
            freed[i] = vdone
        free_pr[2:5] = [free_hn, free_tmp[0], free_tmp[1]]
        hT_read = m

        def pack(h):
            nonlocal pack_last
            s = h % 3
            r0, c = 16 * (h % 8), h // 8
            for n, dst, order in (("q", qp[s], QPART), ("k", kp[s], KPART)):
                for j, p in enumerate(order):
                    last = sp.dma(cp[s], lambda e, n=n, dst=dst, j=j, p=p: e.dma_start(
                        dst[16 * j:16 * j + 16, :], parts[n][r0:r0 + 16, c, p, :]), split[-1], qk_read.get(s))
            pack_of[h] = pack_last = last

        def prior_rows(out, base, banks, extra):
            last = extra
            for q in range(4):
                for bk, c0, p0, n in windows(base + 32 * q):
                    if bk in banks:
                        last = pe(lambda e, q=q, c0=c0, p0=p0, n=n, o=banks[bk]: e.matmul(
                            o[32 * q:32 * q + 32, c0:c0 + n], sel[:, :], mt[:, p0:p0 + n], start=False, stop=True,
                            skip_group_check=True), c_mt, c_sel)
            return last

        p1_last = {}

        def pass1(h, qb, c):
            s = h % 3
            i = c % 2
            m = pe(lambda e: e.matmul(bank[i][:, :], qp[s][0:96, qb * 128:qb * 128 + 128], kp[s][0:96, c * 512:c * 512 + 512],
                                      start=True, stop=True, skip_group_check=True), pack_of[h], free_bank[i])
            m = prior_rows(bank[i], qb * 128, {c: bank[i]}, m)
            r = dve(lambda e: e.tensor_reduce(mx[h % 2][:, qb, c:c + 1], bank[i][:, :], X, ALU.max), m,
                    free_mx[h % 2])
            free_bank[i] = r
            p1_last[h] = r

        def rows(h):
            nonlocal free_pt, free_row, free_pk
            s = h % 3
            t = dve(lambda e: e.tensor_reduce(nm[:, :], mx[h % 2][:, :, :], X, ALU.max, negate=True), p1_last[h])
            free_mx[h % 2] = t
            t = dve(lambda e: e.tensor_copy(pk[:, 0, :], nm[:, :]), t, free_pk)
            t = dve(lambda e: e.tensor_tensor(r1[:, :], nm[:, :], pk[:, 0, :], ALU.subtract), t)
            t = dve(lambda e: e.tensor_copy(pk[:, 1, :], r1[:, :]), t)
            t = dve(lambda e: e.tensor_tensor(pk[:, 2, :], r1[:, :], pk[:, 1, :], ALU.subtract), t)
            ptb = pt[:, :].bitcast(BF16)
            t = pe(lambda e: e.transpose(ptb[0:48, 0:128], pk[:, :, :].rearrange("p a b -> p (a b)"), identb[:, :]), t, idb, free_pt)
            free_pk = t
            t = free_pt = dve(lambda e: e.tensor_copy(row[:, :], ptb[0:48, 0:128]), t, free_row)
            for p in range(3):
                t2 = sp.dma(cr[s], lambda e, p=p: e.dma_start(qp[s][96 + p:97 + p, :], row[16 * p:16 * p + 16, :]), t)
            free_row = row_of[h] = t2

        exps = {}

        def pass2(h, kb, u):
            s = h % 3
            n = (h * W + kb) * 2 + u
            for c in range(2):
                m = pe(lambda e, c=c: e.matmul(wide[u][:, c * 512:c * 512 + 512], kp[s][0:99, kb * 128:kb * 128 + 128],
                                               qp[s][0:99, u * 1024 + c * 512:u * 1024 + c * 512 + 512],
                                               start=True, stop=True, skip_group_check=True), pack_of[h], row_of[h], c_one, free_wide[u])
            qk_read[s] = m
            m = prior_rows(None, kb * 128, {2 * u + c: wide[u][:, c * 512:c * 512 + 512] for c in range(2)}, m)
            x = act(lambda e: e.activation(pr[n % NP][:, :], wide[u][:, :], ACT.Exp, scale=0.25), m, free_pr[n % NP])
            free_wide[u] = exps[n] = x

        def pv(h, kb):
            nonlocal pv_last
            n = (h * W + kb) * 2
            for j in range(4):
                i = (n + j // 2) % NP
                m = pe(lambda e, j=j, i=i: e.matmul(po[32 * j:32 * j + DA + 1, :], v[:, kb, h, :],
                                                    pr[i][:, (j % 2) * 512:(j % 2) * 512 + 512], start=kb == 0, stop=kb == W - 1,
                                                    skip_group_check=True), exps[n + j // 2], free_po if kb == 0 else None, vdone)
                free_pr[i] = m
            pv_last = m

        def finish(h):
            nonlocal free_po, free_osb, free_pt, norm_last
            o = free_po = act(lambda e: e.activation(osb[:, :], po[:, :], ACT.Copy), pv_last, free_osb)
            for s in range(4):
                t = pe(lambda e, s=s: e.transpose(pt[:, s * 128:s * 128 + 128], osb[:, s * 128:s * 128 + 128], ident[:, :]), o, free_pt)
            free_osb = t
            z = pt[:, :].rearrange("p (s j e) -> p s j e", s=4, j=4)
            r = dve(lambda e: e.reciprocal(rc[:, :, :], z[:, :, :, DA]), t)
            norm_last = free_pt = dve(lambda e: e.tensor_tensor(
                at[:, :, h * DA:h * DA + DA].rearrange("p (j s) d -> p s j d", s=4), z[:, :, :, 0:DA],
                rc[:, :, :].unsqueeze(3).to_broadcast([128, 4, 4, DA]), ALU.mult), r, hT_read)

        free_bank[0], free_bank[1] = freed[0], freed[1]
        free_wide[0], free_wide[1] = freed[2:4], freed[4:6]
        LAG = 3
        pack(0)
        pack(1)
        p1 = [(h, qb) for h in range(HA) for qb in range(W)]
        i1 = 0

        def p1_step():
            nonlocal i1
            h, qb = p1[i1]
            for c in range(4):
                yield lambda c=c: pass1(h, qb, c)
            i1 += 1

        def p1_end():
            h, qb = p1[i1 - 1]
            if qb == W - 1:
                rows(h)

        for _ in range(W + LAG):
            for f in p1_step():
                f()
            p1_end()
        for h in range(HA):
            for kb in range(W):
                if kb == 0 and h + 2 < HA:
                    pack(h + 2)
                f = list(p1_step()) if i1 < len(p1) else None
                pass2(h, kb, 0)
                if f:
                    f[0]()
                    f[1]()
                pass2(h, kb, 1)
                if f:
                    f[2]()
                    f[3]()
                    p1_end()
                if kb:
                    pv(h, kb - 1)
                elif h:
                    pv(h - 1, W - 1)
                    finish(h - 1)
        pv(HA - 1, W - 1)
        finish(HA - 1)

        freed = [free_bank[0], free_bank[1], free_wide[0], free_wide[0], free_wide[1], free_wide[1]]
        aT = [p[:, 0:256] for p in pr]
        done = []
        for w in range(W):
            i, bk = slot()
            for c in range(2):
                m = pe(lambda e, c=c, w=w, bk=bk: e.transpose(bk[:, c * 128:c * 128 + 128], at[:, w, c * 128:c * 128 + 128], ident[:, :]),
                       norm_last, freed[i])
            final_reads = m
            s = w % NP
            t = freed[i] = act(lambda e, bk=bk, s=s: e.activation(aT[s], bk[:, 0:256], ACT.Copy), m, free_pr[s], pv_last)
            i, bk = slot()
            for c in range(2):
                m = pe(lambda e, c=c, s=s, bk=bk: e.matmul(bk[:, 0:D], aT[s][:, c * 128:c * 128 + 128], wt["o"][:, c, :],
                                                          start=c == 0, stop=c == 1), t, freed[i])
            free_pr[s] = m
            xt = xs[:, b * W + w, :]
            t = freed[i] = dve(lambda e, bk=bk, xt=xt: e.tensor_tensor(xt, bk[:, 0:D], xt, ALU.add), m)
            t = dve(lambda e, xt=xt: e.tensor_tensor(xt, xt, brow["o"][:, :], ALU.add), t)
            done.append(t)
        x1_done = sp.dma(cs, lambda e, b=b: e.dma_start(x1[b].rearrange("(w p) d -> p w d", p=128), xs[:, b * W:(b + 1) * W, :]), done[-1])
        for w in range(W):
            t = dve(lambda e, w=w, b=b: e.bn_stats(st[:, w, :], xs[:, b * W + w, :]), done[w])
            t = dve(lambda e, w=w: e.bn_aggr(mv[:, w, :], st[:, w, :]), t)
        t = dve(lambda e: e.tensor_scalar(ve[:, :], mv[:, :, 1], EPS, None, ALU.add), t)
        t = pool(lambda e: e.tensor_tensor(rs[:, :], ve[:, :], nh[:, :], ALU.pow), t)
        for w in range(W):
            ln2 = dve(lambda e, w=w, b=b: e.tensor_scalar(xs[:, b * W + w, :], xs[:, b * W + w, :], mv[:, w, 0:1], rs[:, w:w + 1],
                                                         ALU.subtract, ALU.mult), t, x1_done)
    sp(None, x1_done)
    ph.run()


HL, DL = 8, 64
NEG = -3.3895313892515355e38
FC, FW = 6, 114
ROUNDS = [(0, 112), (112, 15)]


def shift(ph, xs, dst, counter, b, waits, zero):
    up = xs[:, b * W:(b + 1) * W, 128:256]
    for p, n in ROUNDS:
        ph.sp.dma(counter, lambda e, p=p, n=n: e.dma_start(dst[p + 1:p + 1 + n, :, :], up[p:p + n, :, :]), waits)
    return ph.sp.dma(counter, lambda e: e.dma_start(dst[0:1, 1:W, :], up[127:128, 0:W - 1, :]), waits, zero)


def rotary():
    half = np.arange(0, DL, 2, dtype=np.float32)
    inv = np.float32(1.0) / np.float32(10000.0) ** (half / np.float32(DL))
    t = np.arange(L, dtype=np.float32)
    f = t[:, None] * inv[None, :]
    f = np.concatenate([f, f], 1)
    base = (half + np.float32(0.4 * DL)) / np.float32(1.4 * DL)
    power = (t - np.float32(L // 2)) / np.float32(64.0)
    s = base[None, :] ** power[:, None]
    s = np.concatenate([s, s], 1)
    sign = np.concatenate([-np.ones(32), np.ones(32)]).astype(np.float32)
    cos, sin = np.cos(f), np.sin(f) * sign
    e = np.float32(8.0)
    q, k = np.stack([cos * s * e, sin * s * e], 1), np.stack([cos / s, sin / s], 1)
    return np.ascontiguousarray(np.stack([q, k], 1).astype(np.float32).reshape(W, 128, 2, 2, DL).transpose(1, 0, 2, 3, 4))


def causal():
    r, c = np.arange(128)[:, None], np.arange(128)[None, :]
    m = np.concatenate([np.where(c >= r, 0.0, NEG), np.where(c <= r, 0.0, NEG)], 1)
    return np.concatenate([m, m], 1).astype(np.float32)


def local_layer(nc, xs, layer, a):
    ph = Phase(nc, f"l{layer}")
    pe, act, dve, pool, sp = ph.pe, ph.act, ph.dve, ph.pool, ph.sp
    sb = ph.sb
    wq = sb("wqkv", [128, 2, 3 * HL * DL])
    wo = sb("wo", [128, 4, D])
    tab = sb("tab", [128, W, 2, 2, DL])
    qsc = sb("qsc", [128, 2, 2, DL])
    ident, identb = sb("ident", [128, 128]), sb("identb", [128, 128], BF16)
    mask32, mask = sb("mask32", [128, 512]), sb("mask", [128, 512], BF16)
    nh = sb("nh", [128, 16])
    sh = [sb(f"sh{i}", [128, W, 128]) for i in range(2)]
    hT = [sb(f"hT{i}", [128, 2, 128]) for i in range(2)]
    qk = [sb(f"qk{i}", [128, 2, HL, DL]) for i in range(2)]
    sq = sb("sq", [128, 2, HL, DL])
    t1 = [sb(f"t1{i}", [128, 2, HL, DL]) for i in range(2)]
    t2 = sb("t2", [128, 2, HL, DL])
    ss, ri = [sb(f"ss{i}", [128, 16]) for i in range(2)], [sb(f"ri{i}", [128, 16]) for i in range(2)]
    qT = [sb(f"qT{i}", [128, 4, 128]) for i in range(2)]
    kT = [sb(f"kT{i}", [128, 4, 2, 128]) for i in range(3)]
    v = [sb(f"v{i}", [128, HL * DL]) for i in range(5)]
    p = [sb(f"p{i}", [128, HL, 2, 128]) for i in range(2)]
    nm, sm, rc = ([sb(f"{n}{i}", [128, HL]) for i in range(2)] for n in ("nm", "sm", "rc"))
    pT = [sb(f"pT{i}", [128, 2, 2, 128]) for i in range(4)]
    oT = [sb(f"oT{i}", [128, 4, 128]) for i in range(2)]
    G = [ph.ps(f"G{i}", [128, 512]) for i in range(2)]
    T = ph.ps("T", [128, 512])
    S = [ph.ps(f"S{i}", [128, 512]) for i in range(2)]
    R = [ph.ps(f"R{i}", [128, 512]) for i in range(2)]
    O = ph.ps("O", [128, 512])

    cw = ph.counter("cw")
    sp.dma(cw, lambda e: e.dma_start(ident[:, :], a["ident"]))
    sp.dma(cw, lambda e: e.dma_start(wq[:, :, :], a["wqkv"][layer].rearrange("(c p) n -> p c n", p=128)))
    sp.dma(cw, lambda e: e.dma_start(tab[:, :, :, :, :], a["rotary"]))
    sp.dma(cw, lambda e: e.dma_start(qsc[:, :, :, :].rearrange("p a b d -> p (a b d)"), a["qsc"][layer].partition_broadcast(128)))
    sp.dma(cw, lambda e: e.dma_start(mask32[:, :], a["causal"]))
    const = sp.dma(cw, lambda e: e.dma_start(wo[:, :, :], a["lwo"][layer].rearrange("(c p) n -> p c n", p=128)))
    zero = [pool(lambda e, i=i: e.memset(sh[i][0:1, 0, :], 0.0)) for i in range(2)]
    csh = [ph.counter(f"sh{i}") for i in range(2)]
    shifted, sh_read = {}, {}
    for b in range(min(2, NB)):
        shifted[b] = shift(ph, xs, sh[b % 2], csh[b % 2], b, None, zero[b % 2])
    c_nh = pool(lambda e: e.memset(nh[:, :], -0.5))
    c_kT = [pool(lambda e, i=i: e.memset(kT[i][:, :, :, :], 0.0)) for i in range(3)]
    idb = dve(lambda e: e.tensor_copy(identb[:, :], ident[:, :]), const)
    c_mask = dve(lambda e: e.tensor_copy(mask[:, :], mask32[:, :]), const)
    c_tab = [dve(lambda e, i=i: e.tensor_tensor(tab[:, :, i, :, :], tab[:, :, i, :, :],
                                                qsc[:, i, :, :].unsqueeze(1).to_broadcast([128, W, 2, DL]), ALU.mult), const)
             for i in range(2)]

    free_G, free_T, free_S, free_R, free_O = [None] * 2, [None], [None] * 2, [None] * 2, [None]
    xT, hTr, qkE, qkR, t1w, t1r, ready = {}, {}, {}, {}, {}, {}, {}
    qTw, qTr, kTw, kTr, vw, vr = {}, {}, {}, {}, {}, {}
    pw, pn, pr, recip, pTr, ow, owr, mxs, tsum = {}, {}, {}, {}, {}, {}, {}, {}, {}
    t2r, sqr, done = [None], [None], {}

    def x_T(t):
        b, w = divmod(t, W)
        src = [xs[:, t, 0:128], sh[b % 2][:, w, :]]
        for c in range(2):
            m = pe(lambda e, c=c: e.transpose(T[:, c * 128:c * 128 + 128], src[c], ident[:, :]), const, shifted[b], free_T[0])
        sh_read[b] = m
        xT[t] = free_T[0] = act(lambda e: e.activation(hT[t % 2][:, :, :].rearrange("p c n -> p (c n)"), T[:, 0:256], ACT.Copy),
                                m, hTr.get(t - 2))

    def qkv(t, n):
        g = G[n % 2]
        for c in range(2):
            m = pe(lambda e, c=c: e.matmul(g[:, :], hT[t % 2][:, c, :], wq[:, c, n * 512:n * 512 + 512], start=c == 0, stop=c == 1),
                   xT[t], free_G[n % 2])
        hTr[t] = m
        if n < 2:
            free_G[n] = qkE[t, n] = act(lambda e: e.activation(qk[t % 2][:, n, :, :].rearrange("p h d -> p (h d)"), g[:, :], ACT.Copy),
                                        m, qkR.get(t - 2))
        else:
            free_G[0] = vw[t] = act(lambda e: e.activation(v[t % 5][:, :], g[:, :], ACT.Copy), m, vr.get(t - 5))

    def rotate(t):
        s = t % 2
        src, w = qk[s], t % W
        sw = act(lambda e: e.activation(sq[:, :, :, :], src[:, :, :, :], ACT.Square),
                  qkE[t, 0], qkE[t, 1], sqr[0])
        a1 = dve(lambda e: e.tensor_tensor(t1[s][:, :, :, :], src[:, :, :, :],
                                           tab[:, w, :, 0, :].unsqueeze(2).to_broadcast([128, 2, HL, DL]), ALU.mult),
                 qkE[t, 0], qkE[t, 1], c_tab, t1r.get(t - 2))
        for i in range(2):
            a2 = dve(lambda e, i=i: e.tensor_tensor(
                t2[:, :, :, 32 * i:32 * i + 32], src[:, :, :, 32 - 32 * i:64 - 32 * i],
                tab[:, w, :, 1, 32 * i:32 * i + 32].unsqueeze(2).to_broadcast([128, 2, HL, 32]), ALU.mult), t2r[0])
        sqr[0] = r = dve(lambda e: e.tensor_reduce(ss[s][:, :], sq[:, :, :, :].rearrange("p a h d -> p (a h) d"), X, ALU.add), sw, t1r.get(t - 2))
        qkR[t] = [sw, a2]
        r = dve(lambda e: e.tensor_scalar(ss[s][:, :], ss[s][:, :], 1e-24, None, ALU.max), r)
        r = pool(lambda e: e.tensor_tensor(ri[s][:, :], ss[s][:, :], nh[:, :], ALU.pow), r, c_nh)
        t2r[0] = q = pool(lambda e: e.tensor_tensor(t1[s][:, :, :, :], t1[s][:, :, :, :], t2[:, :, :, :], ALU.add), a1, a2)
        flat_ = t1[s][:, :, :, :].rearrange("p a h d -> p (a h) d")
        ready[t] = dve(lambda e: e.tensor_tensor(flat_, flat_, ri[s][:, :].unsqueeze(2).to_broadcast([128, 16, DL]), ALU.mult), q, r)

    def qk_T(t, n):
        for i in range(4):
            m = pe(lambda e, i=i: e.transpose(T[:, i * 128:i * 128 + 128],
                                              t1[t % 2][:, n, 2 * i:2 * i + 2, :].rearrange("p h d -> p (h d)"), ident[:, :]),
                   ready[t], free_T[0])
        t1r[t] = m
        if n == 0:
            free_T[0] = qTw[t] = act(lambda e: e.activation(qT[t % 2][:, :, :].rearrange("p a n -> p (a n)"), T[:, :], ACT.Copy), m, qTr.get(t - 2))
        else:
            for i in range(2):
                z = dve(lambda e, i=i: e.tensor_copy(kT[t % 3][64 * i:64 * i + 64, :, i, :],
                                                     T[64 * i:64 * i + 64, :].rearrange("p (a n) -> p a n", a=4)),
                        m, c_kT, kTr.get(t - 3), kTr.get(t - 2))
            free_T[0] = kTw[t] = z

    def sim(t, pair):
        w, s = t % W, S[pair % 2]
        z = s[:, :].rearrange("p (h k n) -> p h k n", h=2, k=2)
        pe(lambda e: e.matmul(s[:, :], identb[:, :], mask[:, :], start=True, stop=False, skip_group_check=True),
           idb, c_mask, free_S[pair % 2])
        for k in ([0, 1] if w else [1]):
            m = pe(lambda e, k=k: e.matmul(z[:, :, k, :], qT[t % 2][:, pair, :], kT[(t - 1 + k) % 3][:, pair, :, :],
                                           start=False, stop=True, skip_group_check=True), qTw[t], kTw[t])
        qTr[t] = kTr[t] = m
        x = dve(lambda e: e.tensor_reduce(nm[t % 2][:, 2 * pair:2 * pair + 2], s[:, :].rearrange("p (h k) -> p h k", h=2) if w else z[:, :, 1, :],
                                          X, ALU.max, negate=True), m, pw.get((t - 2, pair)))
        for h in range(2):
            hh = 2 * pair + h
            dst = p[t % 2][:, hh, :, :].rearrange("p k n -> p (k n)") if w else p[t % 2][:, hh, 1, :]
            src = s[:, h * 256:h * 256 + 256] if w else z[:, h, 1, :]
            y = act(lambda e, hh=hh, dst=dst, src=src: e.activation(dst, src, ACT.Exp, bias=nm[t % 2][:, hh:hh + 1],
                                                                    accum_out=sm[t % 2][:, hh:hh + 1]),
                    x, pr.get((t - 2, pair)), recip.get(t - 2))
        free_S[pair % 2] = pw[t, pair] = y

    def normalise(t):
        w = t % W
        recip[t] = r = dve(lambda e: e.reciprocal(rc[t % 2][:, :], sm[t % 2][:, :]), pw[t, 3], pn.get((t - 2, 3)))
        for pair in range(4):
            z = p[t % 2][:, 2 * pair:2 * pair + 2, :, :]
            z = z.rearrange("p h k n -> p h (k n)") if w else z[:, :, 1, :]
            pn[t, pair] = pool(lambda e, z=z, pair=pair: e.tensor_tensor(
                z, z, rc[t % 2][:, 2 * pair:2 * pair + 2].unsqueeze(2).to_broadcast([128, 2, 256 if w else 128]), ALU.mult), r)

    def p_T(t, pair):
        w, r = t % W, R[pair % 2]
        ks = [0, 1] if w else [1]
        for h in range(2):
            for k in ks:
                m = pe(lambda e, h=h, k=k: e.transpose(r[:, (2 * k + h) * 128:(2 * k + h) * 128 + 128], p[t % 2][:, 2 * pair + h, k, :], ident[:, :]),
                       pn[t, pair], free_R[pair % 2])
        pr[t, pair] = m
        dst = pT[pair][:, :, :, :].rearrange("p k h n -> p (k h n)")
        lo = 0 if w else 256
        if pair % 2:
            free_R[1] = y = dve(lambda e: e.tensor_copy(dst[:, lo:512], r[:, lo:512]), m, pTr.get(pair))
        else:
            free_R[0] = y = act(lambda e: e.activation(dst[:, lo:512], r[:, lo:512], ACT.Copy), m, pTr.get(pair))
        ks = ks
        pw[t, pair, "T"] = y

    def pv(t, pair):
        w = t % W
        for k in ([0, 1] if w else [1]):
            for h in range(2):
                hh = 2 * pair + h
                m = pe(lambda e, h=h, k=k, hh=hh: e.matmul(
                    O[64 * h:64 * h + 64, pair * 128:pair * 128 + 128], v[(t - 1 + k) % 5][:, hh * DL:hh * DL + DL], pT[pair][:, k, h, :],
                    start=k == 0 or w == 0, stop=k == 1, skip_group_check=True), pw[t, pair, "T"], vw[t], free_O[0])
        pTr[pair] = vr[t - 1] = m
        if pair == 3:
            free_O[0] = ow[t] = act(lambda e: e.activation(oT[t % 2][:, :, :].rearrange("p a n -> p (a n)"), O[:, :], ACT.Copy), m, owr.get(t - 2))

    def out(t):
        for c in range(4):
            m = pe(lambda e, c=c: e.matmul(G[1][:, 0:D], oT[t % 2][:, c, :], wo[:, c, :], start=c == 0, stop=c == 3), ow[t], free_G[1])
        owr[t] = m
        b = t // W
        done[t] = free_G[1] = dve(lambda e: e.tensor_tensor(xs[:, t, :], G[1][:, 0:D], xs[:, t, :], ALU.add), m, shifted[b])

    def on(f, t, *args):
        if 0 <= t < NT:
            f(t, *args)

    on(x_T, 0)
    for n in range(NT + 4):
        on(sim, n - 2, 0)
        on(qkv, n, 0)
        on(sim, n - 2, 1)
        on(qkv, n, 1)
        on(rotate, n)
        on(p_T, n - 3, 0)
        on(sim, n - 2, 2)
        on(qkv, n, 2)
        on(p_T, n - 3, 1)
        on(qk_T, n - 1, 0)
        on(pv, n - 3, 0)
        on(sim, n - 2, 3)
        on(normalise, n - 2)
        on(p_T, n - 3, 2)
        on(pv, n - 3, 1)
        on(qk_T, n - 1, 1)
        on(p_T, n - 3, 3)
        on(pv, n - 3, 2)
        if (n + 1) % W == 0 and 0 <= (n + 1) // W - 2 and (n + 1) // W < NB:
            pass
        if n + 1 < NT:
            b = (n + 1) // W
            if b not in shifted:
                shifted[b] = shift(ph, xs, sh[b % 2], csh[b % 2], b, [sh_read[b - 2]], zero[b % 2])
        on(x_T, n + 1)
        on(pv, n - 3, 3)
        on(out, n - 4)
    ph.run()


def feed_forward(nc, xs, layer, last, x1, y, a):
    ph = Phase(nc, f"f{layer}")
    pe, act, dve, pool, sp = ph.pe, ph.act, ph.dve, ph.pool, ph.sp
    sb = ph.sb
    NG = NT // 4
    w1 = sb("w1", [128, 2, 2 * FC * FW])
    w2 = sb("w2", [FW, FC, D])
    b1 = sb("b1", [FW, 2 * FC])
    lg, lb = sb("lg", [128, 2]), sb("lb", [128, 2])
    b2 = sb("b2", [128, D])
    ident = sb("ident", [128, 128])
    nh = sb("nh", [128, W])
    sh = [sb(f"sh{i}", [128, W, 128]) for i in range(2)]
    st = [sb(f"st{i}", [128, W, 2, 6]) for i in range(2)]
    mv = [sb(f"mv{i}", [128, W, 2]) for i in range(2)]
    ve, rs = [sb(f"ve{i}", [128, W]) for i in range(2)], [sb(f"rs{i}", [128, W]) for i in range(2)]
    hn = [sb(f"hn{i}", [128, D]) for i in range(4)]
    hT = [sb(f"hT{i}", [128, 2, 512]) for i in range(2)]
    gg = [sb(f"gg{i}", [FW, 512]) for i in range(2)]
    u = [sb(f"u{i}", [FW, FC, 512]) for i in range(2)]
    xo = [sb(f"xo{i}", [128, 4, D]) for i in range(2)] if last else None
    T = [ph.ps(f"T{i}", [128, 512]) for i in range(2)]
    F = [ph.ps(f"F{i}", [128, 512]) for i in range(4)]
    Y = [ph.ps(f"Y{i}", [128, 512]) for i in range(2)]

    cw = ph.counter("cw")
    sp.dma(cw, lambda e: e.dma_start(w1[:, :, :], a["w1"][layer].rearrange("(c p) n -> p c n", p=128)))
    sp.dma(cw, lambda e: e.dma_start(w2[:, :, :], a["w2"][layer].rearrange("(c p) n -> p c n", p=FW)))
    for d, n in ((b1, "b1"), (lg, "lg"), (lb, "lb")):
        sp.dma(cw, lambda e, d=d, n=n: e.dma_start(d[:, :], a[n][layer]))
    sp.dma(cw, lambda e: e.dma_start(b2[:, :], a["b2"][layer].partition_broadcast(128)))
    const = sp.dma(cw, lambda e: e.dma_start(ident[:, :], a["ident"]))
    zero = [pool(lambda e, i=i: e.memset(sh[i][0:1, 0, :], 0.0)) for i in range(2)]
    csh = [ph.counter(f"sh{i}") for i in range(2)]
    cx, cy = [ph.counter(f"x{i}") for i in range(2)], ph.counter("y")
    shifted, sh_read = {}, {}
    for b in range(min(2, NB)):
        shifted[b] = shift(ph, xs, sh[b % 2], csh[b % 2], b, None, zero[b % 2])
    c_nh = pool(lambda e: e.memset(nh[:, :], -0.5))

    for j in range(2 * FC):
        for c in range(2):
            m = pe(lambda e, j=j, c=c: e.matmul(F[3][0:FW, j:j + 1], w1[:, c, j * FW:j * FW + FW], lb[:, c:c + 1],
                                                start=c == 0, stop=c == 1, skip_group_check=True), const)
    c_b1 = dve(lambda e: e.tensor_tensor(b1[:, :], F[3][0:FW, 0:2 * FC], b1[:, :], ALU.add), m)
    for c in range(2):
        c_w1 = dve(lambda e, c=c: e.tensor_scalar(w1[:, c, :], w1[:, c, :], lg[:, c:c + 1], None, ALU.mult), m)

    free_T, free_F, free_Y = [None] * 2, [None, None, None, c_b1], [None] * 2
    free_hn, hTw, hTr, uw, ur, free_gg, stats, xin, xor_, done = [None] * 4, {}, {}, {}, {}, [None] * 2, {}, {}, {}, {}

    def statistics(b):
        s = b % 2
        prev = sh_read.get(b - 2)
        for w in range(W):
            dve(lambda e, w=w: e.bn_stats(st[s][:, w, 0, :], xs[:, b * W + w, 0:128]), shifted[b])
            t = dve(lambda e, w=w: e.bn_stats(st[s][:, w, 1, :], sh[s][:, w, :]), shifted[b])
            t = dve(lambda e, w=w: e.bn_aggr(mv[s][:, w, :], st[s][:, w, :, :].rearrange("p a b -> p (a b)")), t)
        t = dve(lambda e: e.tensor_scalar(ve[s][:, :], mv[s][:, :, 1], EPS, None, ALU.add), t)
        stats[b] = pool(lambda e: e.tensor_tensor(rs[s][:, :], ve[s][:, :], nh[:, :], ALU.pow), t, c_nh)

    def normal_T(g, i):
        t = 4 * g + i
        b, w = divmod(t, W)
        s = b % 2
        for c, src in enumerate((xs[:, t, 0:128], sh[s][:, w, :])):
            n = dve(lambda e, c=c, src=src: e.tensor_scalar(hn[i][:, c * 128:c * 128 + 128], src, mv[s][:, w, 0:1], rs[s][:, w:w + 1],
                                                            ALU.subtract, ALU.mult), stats[b], free_hn[i])
        sh_read[b] = n
        for c in range(2):
            m = pe(lambda e, c=c: e.transpose(T[c][:, i * 128:i * 128 + 128], hn[i][:, c * 128:c * 128 + 128], ident[:, :]),
                   n, const, free_T[c] if i == 0 else None)
        free_hn[i] = m
        if i == 3:
            for c in range(2):
                free_T[c] = hTw[g] = act(lambda e, c=c: e.activation(hT[g % 2][:, c, :], T[c][:, :], ACT.Copy), m, hTr.get(g - 2))

    def hidden(g, j):
        fa, fg = F[2 * (j % 2)], F[2 * (j % 2) + 1]
        for f, k, o in ((fa, j, 0), (fg, FC + j, 1)):
            for c in range(2):
                m = pe(lambda e, c=c, f=f, k=k: e.matmul(f[0:FW, :], w1[:, c, k * FW:k * FW + FW], hT[g % 2][:, c, :],
                                                         start=c == 0, stop=c == 1), hTw[g], c_w1, free_F[2 * (j % 2) + o])
        hTr[g] = m
        x = free_F[2 * (j % 2) + 1] = act(lambda e: e.activation(gg[j % 2][:, :], fg[0:FW, :], ACT.Gelu, bias=b1[:, FC + j:FC + j + 1]),
                                          m, c_b1, free_gg[j % 2])
        x = dve(lambda e: e.scalar_tensor_tensor(u[g % 2][:, j, :], fa[0:FW, :], b1[:, j:j + 1], gg[j % 2][:, :], ALU.add, ALU.mult),
                x, ur.get(g - 2))
        free_F[2 * (j % 2)] = free_gg[j % 2] = uw[g, j] = x

    def out(g, i):
        t = 4 * g + i
        for j in range(FC):
            m = pe(lambda e, j=j: e.matmul(Y[i % 2][:, 0:D], u[g % 2][:, j, i * 128:i * 128 + 128], w2[:, j, :],
                                           start=j == 0, stop=j == FC - 1), uw[g, j], free_Y[i % 2])
        ur[g] = m
        b = t // W
        z = free_Y[i % 2] = dve(lambda e: e.tensor_tensor(xs[:, t, :], Y[i % 2][:, 0:D], xs[:, t, :], ALU.add), m, shifted[b])
        z = dve(lambda e: e.tensor_tensor(xs[:, t, :], xs[:, t, :], b2[:, :], ALU.add), z)
        if last:
            z = pool(lambda e: e.tensor_tensor(xs[:, t, :], xs[:, t, :], xo[g % 2][:, i, :], ALU.add), z, xin[g])
            if i == 3:
                xor_[g] = z
                b, w = divmod(4 * g, W)
                done[g] = sp.dma(cy, lambda e: e.dma_start(y[b, w * 128:w * 128 + 512, :].rearrange("(w p) d -> p w d", p=128),
                                                           xs[:, 4 * g:4 * g + 4, :]), z)

    def fetch(g):
        b, w = divmod(4 * g, W)
        xin[g] = sp.dma(cx[g % 2], lambda e: e.dma_start(xo[g % 2][:, :, :], x1[b, w * 128:w * 128 + 512, :].rearrange("(w p) d -> p w d", p=128)),
                        xor_.get(g - 2))

    statistics(0)
    for i in range(4):
        normal_T(0, i)
    for g in range(NG + 1):
        if last and g < NG:
            fetch(g)
        b = (4 * (g + 1)) // W
        if g + 1 < NG and (4 * (g + 1)) % W == 0 and b not in shifted:
            shifted[b] = shift(ph, xs, sh[b % 2], csh[b % 2], b, [sh_read[b - 2]], zero[b % 2])
        if g + 1 < NG and b not in stats:
            statistics(b)
        for j in range(FC):
            if g < NG:
                hidden(g, j)
            if g and j in (1, 2, 3, 4):
                out(g - 1, j - 1)
            if g + 1 < NG and j in (1, 2, 3, 4):
                normal_T(g + 1, j - 1)
    if last:
        sp(None, done[NG - 1])
    ph.run()


def program(nc, a, y):
    x1 = nc.dram_tensor("x1", [NB, L, D], F32, kind="Internal").ap()
    with nc.sbuf_tensor("xs", [128, NT, D], F32) as xs:
        attention(nc, xs, x1, a)
        for layer in range(2):
            local_layer(nc, xs, layer, a)
            feed_forward(nc, xs, layer, layer == 1, x1, y, a)


def kernel(**inputs):
    import concourse.bacc as bacc
    from concourse.bass_utils import run_bass_kernel_spmd

    i = {k.removeprefix("L0_"): np.asarray(x) for k, x in inputs.items()}
    pad = lambda x, axis: np.concatenate([x, np.zeros([FW * FC - 682 if k == axis else n for k, n in enumerate(x.shape)], x.dtype)], axis)
    halves = lambda x, axis: np.concatenate([pad(h, axis) for h in np.split(x, 2, axis)], axis)
    two = lambda x: np.stack(np.split(x, 2, -1), -1)
    swap = lambda x: np.concatenate([x[:, 32:], x[:, :32]], 1)
    qs, ks = i["ffn_q_scale"], i["ffn_k_scale"]
    arrays = dict(
        x=i["attn_x"], wq=i["attn_Wq"].T, wk=i["attn_Wk"].T, wv=i["attn_Wv"].T, wo=i["attn_Wo"].T,
        bq=two(i["attn_bq"]), bk=two(i["attn_bk"]), bv=i["attn_bv"], bo=i["attn_bo"], lam=i["attn_prior_lambda"].reshape(1),
        prior=prior(), sel=np.concatenate([np.eye(32, dtype=np.float32)] * 3), ident=np.eye(128, dtype=np.float32),
        wqkv=i["ffn_wqkv"], lwo=i["ffn_wo"], rotary=rotary(), causal=causal(),
        qsc=np.concatenate([qs, swap(qs), ks, swap(ks)], 1),
        w1=halves(i["ffn_w1"], 2), b1=halves(i["ffn_b1"], 1).reshape(2, 2 * FC, FW).transpose(0, 2, 1),
        w2=pad(i["ffn_w2"], 1), b2=i["ffn_b2"], lg=two(i["ffn_ln_g"]), lb=two(i["ffn_ln_b"]))
    nc = bacc.Bacc("TRN2", target_bir_lowering=False, num_devices=1)
    given, a = {}, {}
    for name, x in arrays.items():
        given["in_" + name] = x = np.ascontiguousarray(x)
        a[name] = nc.dram_tensor("in_" + name, x.shape, mybir.dt.from_np(x.dtype), kind="ExternalInput").ap()
    y = nc.dram_tensor("out", (NB, L, D), F32, kind="ExternalOutput").ap()
    program(nc, a, y)
    r = run_bass_kernel_spmd(nc, [given], core_ids=[0])
    return r.results[0]["out"]
```

```python
from contextlib import ExitStack

import numpy as np
import concourse.bass as bass
from concourse import mybir

F32 = mybir.dt.float32
BF16 = mybir.dt.bfloat16
F32R = mybir.dt.float32r
ALU = mybir.AluOpType
ACT = mybir.ActivationFunctionType
X = mybir.AxisListType.X

NB, L, D = 4, 2048, 256
W = L // 128
NT = NB * W
EPS = 1e-5
HA, DA = 16, 16
BAND = 59
WIN = 32 + 2 * BAND
WIDE0 = 512
QPART = [0, 1, 2, 0, 1, 0]
KPART = [0, 0, 0, 1, 1, 2]


class Op:
    def __init__(self, lane, fn, waits, sem=None, val=None):
        self.lane, self.fn, self.waits = lane, fn, waits
        self.sem, self.val, self.signals, self.dma = sem, val, False, sem is not None


def flat(waits):
    out = []
    for w in waits:
        out += flat(w) if isinstance(w, (list, tuple)) else [] if w is None else [w]
    return out


class Lane:

    def __init__(self, sem):
        self.sem, self.ops = sem, []

    def __call__(self, fn, *waits):
        op = Op(self, fn, flat(waits))
        for w in op.waits:
            w.signals = True
        self.ops.append(op)
        return op

    def dma(self, counter, fn, *waits):
        counter.n += 16
        op = Op(self, fn, flat(waits), counter.sem, counter.n)
        for w in op.waits:
            w.signals = True
        self.ops.append(op)
        return op

    def number(self):
        n = 0
        for op in self.ops:
            if op.signals and not op.dma:
                n += 1
                op.sem, op.val = self.sem, n

    def emit(self, eng):
        seen = {}
        for op in self.ops:
            need = {}
            for w in op.waits:
                need[w.sem] = max(need.get(w.sem, 0), w.val)
            for s, v in need.items():
                if seen.get(s, 0) < v:
                    eng.wait_ge(s, v)
                    seen[s] = v
            inst = op.fn and op.fn(eng)
            if op.dma:
                inst.then_inc(op.sem, 16)
            elif op.signals:
                inst.then_inc(op.sem, 1)


class Counter:

    def __init__(self, sem):
        self.sem, self.n = sem, 0


class Phase:

    def __init__(self, nc, tag):
        self.nc, self.tag, self.ctx = nc, tag, ExitStack()
        self.pe, self.act, self.dve, self.pool, self.sp = (Lane(self.sem(n)) for n in ("pe", "act", "dve", "pool", "sp"))

    def sem(self, name):
        return self.ctx.enter_context(self.nc.semaphore(f"{self.tag}_{name}"))

    def counter(self, name):
        return Counter(self.sem(name))

    def sb(self, name, shape, dt=F32):
        return self.ctx.enter_context(self.nc.sbuf_tensor(f"{self.tag}_{name}", shape, dt))

    def ps(self, name, shape, dt=F32):
        return self.ctx.enter_context(self.nc.psum_tensor(f"{self.tag}_{name}", shape, dt))

    def run(self):
        lanes = dict(tensor=self.pe, scalar=self.act, vector=self.dve, gpsimd=self.pool, sync=self.sp)
        for lane in lanes.values():
            lane.number()
        with self.nc.Block() as block:
            for name, lane in lanes.items():
                def body(eng, lane=lane):
                    lane.emit(eng)
                {"tensor": block.tensor, "scalar": block.scalar, "vector": block.vector,
                 "gpsimd": block.gpsimd, "sync": block.sync}[name](body)
        self.ctx.close()


def prior():
    i, c = np.arange(32, dtype=np.float32)[:, None], np.arange(WIN, dtype=np.float32)[None, :]
    delta = np.abs(c - np.float32(BAND) - i)
    g = np.zeros_like(delta)
    for p, w, s in ((1.0, 0.8, 0.5), (30.0, 0.4, 2.0)):
        g = g + np.float32(w) * np.exp(-(delta - np.float32(p)) ** 2 / np.float32(2.0 * s * s))
    g[delta > BAND] = 0.0
    return np.concatenate([g, g, g]).astype(np.float32)


def wide_prior():
    d = np.arange(512 + WIDE0 + 128) - WIDE0 - np.arange(128)[:, None]
    one = prior()[0]
    g = np.zeros(d.shape, np.float32)
    near = np.abs(d) <= BAND
    g[near] = one[d[near] + BAND]
    return g


def windows(r0):
    a, e = max(r0 - BAND, 0), min(r0 - BAND + WIN, L)
    while a < e:
        z = min(e, (a // 512 + 1) * 512)
        yield a // 512, a % 512, a - (r0 - BAND), z - a
        a = z


def attention(nc, xs, x1, a):
    ph = Phase(nc, "a")
    pe, act, dve, pool, sp = ph.pe, ph.act, ph.dve, ph.pool, ph.sp
    sb = ph.sb
    at = xs[:, (NB - 1) * W:NB * W, :]
    parts = {"q": sb("qs", [128, 3, L], BF16), "k": sb("ks", [128, 3, L], BF16)}
    qp = [sb(f"qp{i}", [128, L], BF16) for i in range(3)]
    kp = [sb(f"kp{i}", [128, L], BF16) for i in range(3)]
    v = [sb(f"v{i}", [128, W, HA, DA + 1]) for i in range(2)]
    NP = 4
    pr = [sb(f"pr{i}", [128, 1024]) for i in range(NP)]
    xc = [sb(f"xc{i}", [128, 4, D]) for i in range(2)]
    hT = [sb(f"hT{i}", [128, 2, 512]) for i in range(2)]
    wt = {n: sb("w" + n, [128, 2, D]) for n in "qkvo"}
    bias = {n: sb("b" + n, [128, 2]) for n in "qk"}
    brow = {n: sb("r" + n, [128, D]) for n in "vo"}
    ident = sb("ident", [128, 128])
    identb = sb("identb", [128, 128], BF16)
    gt = sb("gt", [96, WIN])
    gp = [sb(f"gp{i}", [96, WIN], BF16) for i in range(3)]
    mt = sb("mt", [96, WIN], BF16)
    gw = sb("gw", [128, 512 + WIDE0 + 128])
    tmp = [sb(f"tmp{i}", [128, 512]) for i in range(2)]
    g1, g2 = tmp[0][0:96, 0:WIN], tmp[1][0:96, 0:WIN]
    osb = sb("osb", [128, 512])
    junk = sb("junk", [128, 512], BF16)
    sel = sb("sel", [96, 32], BF16)
    self32 = sb("self32", [96, 32])
    lam, lam4 = sb("lam", [128, 1]), sb("lam4", [128, 1])
    nh = sb("nh", [128, 4])
    st = sb("st", [128, 4, 6])
    mv, mv2 = sb("mv", [128, W, 2]), sb("mv2", [128, 4, 2])
    rs, rs2 = sb("rs", [128, W]), sb("rs2", [128, 4])
    ve = sb("ve", [128, 4])
    mx = [sb(f"mx{i}", [128, W, 4]) for i in range(2)]
    nm, r1 = sb("nm", [128, W]), sb("r1", [128, W])
    pk = sb("pk", [128, 3, W], BF16)
    row = sb("row", [48, 128], BF16)
    rc = sb("rc", [128, 4, 4])
    bank = [ph.ps(f"b{i}", [128, 512]) for i in range(2)]
    wide = [ph.ps(f"w{i}", [128, 1024]) for i in range(2)]
    po = ph.ps("po", [128, 512])
    pt = ph.ps("pt", [128, 512])

    cw = ph.counter("cw")
    cl, cs = [ph.counter(f"x{i}") for i in range(2)], [ph.counter(f"res{i}") for i in range(2)]
    chunks = []
    for b in range(NB):
        if b == 0:
            chunks += [(0, "v", j) for j in range(4)] + [(0, 0, j) for j in range(4)]
        if b:
            chunks += [(b - 1, "o", j) for j in range(4)]
        chunks += [(b, 1, j) for j in range(4)]
        if b + 1 < NB:
            chunks += [(b + 1, "v", j) for j in range(4)] + [(b + 1, 0, j) for j in range(4)]
    chunks += [(NB - 1, "o", j) for j in range(4)]
    where = {c: k for k, c in enumerate(chunks)}
    loaded, released = {}, {}

    def load(k):
        if k < len(chunks):
            b, _, j = chunks[k]
            loaded[k] = sp.dma(cl[k % 2], lambda e: e.dma_start(
                xc[k % 2][:, :, :], a["x"][b, j * 512:j * 512 + 512, :].rearrange("(w p) d -> p w d", p=128)), released.get(k - 2))

    load(0)
    load(1)
    for n in "vqko":
        sp.dma(cw, lambda e, n=n: e.dma_start(wt[n][:, :, :], a["w" + n].rearrange("(c p) n -> p c n", p=128)))
    for n in "qk":
        sp.dma(cw, lambda e, n=n: e.dma_start(bias[n][:, :], a["b" + n]))
    for n in "vo":
        sp.dma(cw, lambda e, n=n: e.dma_start(brow[n][:, :], a["b" + n].partition_broadcast(128)))
    sp.dma(cw, lambda e: e.dma_start(lam[:, :], a["lam"].partition_broadcast(128)))
    sp.dma(cw, lambda e: e.dma_start(gt[:, :], a["prior"]))
    sp.dma(cw, lambda e: e.dma_start(self32[:, :], a["sel"]))
    sp.dma(cw, lambda e: e.dma_start(gw[:, :], a["wide"]))
    const = sp.dma(cw, lambda e: e.dma_start(ident[:, :], a["ident"]))

    c_nh = pool(lambda e: e.memset(nh[:, :], -0.5))
    for i in range(3):
        c_one = dve(lambda e, i=i: e.memset(kp[i][96:99, :], 1.0))
    for i in range(2):
        c_v1 = pool(lambda e, i=i: e.memset(v[i][:, :, :, DA:DA + 1], 1.0))
    c_po = dve(lambda e: e.memset(po[:, :], 0.0))

    def constants():
        nonlocal idb, c_sel, c_gw, c_mt
        idb = dve(lambda e: e.tensor_copy(identb[:, :], ident[:, :]), const)
        c_sel = dve(lambda e: e.tensor_copy(sel[:, :], self32[:, :]), const)
        t = dve(lambda e: e.tensor_scalar(lam4[:, :], lam[:, :], 4.0, None, ALU.mult), const)
        c_gw = dve(lambda e: e.tensor_scalar(gw[:, :], gw[:, :], lam4[:, :], None, ALU.mult), t)
        t = dve(lambda e: e.tensor_scalar(gt[:, :], gt[:, :], lam4[0:96, :], None, ALU.mult), t)
        t = dve(lambda e: e.tensor_copy(gp[0][:, :], gt[:, :]), t)
        t = dve(lambda e: e.tensor_tensor(g1, gt[:, :], gp[0][:, :], ALU.subtract), t, free_tmp[0])
        t = dve(lambda e: e.tensor_copy(gp[1][:, :], g1), t)
        t = dve(lambda e: e.tensor_tensor(g2, g1, gp[1][:, :], ALU.subtract), t, free_tmp[1])
        t = dve(lambda e: e.tensor_copy(gp[2][:, :], g2), t)
        free_tmp[0] = free_tmp[1] = t
        for i in range(3):
            c_mt = dve(lambda e, i=i: e.tensor_copy(mt[32 * i:32 * i + 32, :], gp[i][32 * i:32 * i + 32, :]), t)

    idb = c_sel = c_gw = c_mt = None
    scratch = [pt[:, :], bank[0][:, :], bank[1][:, :]] + [wide[i][:, c:c + 512] for i in range(2) for c in (0, 512)]
    freed = [None] * 7
    scratch_n, turn = 7, 0

    def slot():
        nonlocal turn
        turn += 1
        i = turn % scratch_n
        return i, scratch[i]

    cp = [ph.counter(f"pack{i}") for i in range(3)]
    cr = [ph.counter(f"row{i}") for i in range(3)]
    pack_of, row_of, qk_read = {}, {}, {}
    free_bank, free_wide = [None] * 2, [None] * 2
    free_pr, free_tmp, free_mx, free_hT = [None] * NP, [None] * 2, [None] * 2, [None] * 2
    free_po, free_osb, free_row, free_pk = c_po, None, None, None
    pk_done, osb_done, norm_last, at_read, junk_w, n_tmp, n_hT, mv2_read, mv_read = None, None, None, None, None, 0, 0, None, None
    pv_last, v_done, pack_last, part_done, mean, normed, hTw, aTw, x1_done = {}, {}, None, {}, {}, {}, {}, {}, {}

    def stats(b, j):
        k = where[b, "v", j]
        for i in range(4):
            t = dve(lambda e, i=i: e.bn_stats(st[:, i, :], xc[k % 2][:, i, :]), loaded[k])
        for i in range(4):
            t = dve(lambda e, i=i: e.bn_aggr(mv[:, 4 * j + i, :], st[:, i, :]), t, mv_read)
        t = dve(lambda e: e.tensor_scalar(ve[:, :], mv[:, 4 * j:4 * j + 4, 1], EPS, None, ALU.add), t)
        mean[b, j] = pool(lambda e: e.tensor_tensor(rs[:, 4 * j:4 * j + 4], ve[:, :], nh[:, :], ALU.pow), t, c_nh)

    def normal(b, kind, j, half):
        nonlocal mv_read
        k = where[b, kind, j]
        for i in (2 * half, 2 * half + 1):
            w = 4 * j + i
            normed[b, kind, j, half] = mv_read = dve(lambda e, i=i, w=w: e.tensor_scalar(
                xc[k % 2][:, i, :], xc[k % 2][:, i, :], mv[:, w, 0:1], rs[:, w:w + 1], ALU.subtract, ALU.mult), mean[b, j], loaded[k])

    def turned(b, kind, j, half):
        nonlocal n_hT
        k = where[b, kind, j]
        if half == 0:
            n_hT += 1
        dst = hT[n_hT % 2]
        s, bk = slot()
        for i in (2 * half, 2 * half + 1):
            for c in range(2):
                m = pe(lambda e, i=i, c=c: e.transpose(bk[:, c * 256 + (i % 2) * 128:c * 256 + (i % 2) * 128 + 128],
                                                       xc[k % 2][:, i, c * 128:c * 128 + 128], ident[:, :]),
                       normed[b, kind, j, half], freed[s], const)
        released[k] = m
        hTw[b, kind, j] = freed[s] = act(lambda e: e.activation(dst[:, :, half * 256:half * 256 + 256],
                                                               bk.rearrange("p (c n) -> p c n", c=2), ACT.Copy), m, free_hT[n_hT % 2])
        if half == 1:
            load(k + 2)

    def project(b, c, j, n):
        nonlocal n_tmp
        src, q = hT[n_hT % 2], n_hT % 2
        s, bk = slot()
        for cc in range(2):
            m = pe(lambda e, cc=cc: e.matmul(bk, wt[n][:, cc, c * 128:c * 128 + 128], src[:, cc, :], start=cc == 0, stop=cc == 1),
                   hTw[b, c, j], freed[s])
        free_hT[q] = m
        d = [parts[n][:, p, j * 512:j * 512 + 512] for p in range(3)]
        i = n_tmp % 2
        tm = tmp[i][:, :]
        n_tmp += 1
        h0 = act(lambda e: e.activation(d[0], bk, ACT.Identity, bias=bias[n][:, c:c + 1]), m, pack_last)

        def rest():
            r = freed[s] = dve(lambda e: e.scalar_tensor_tensor(tm, bk, bias[n][:, c:c + 1], d[0], ALU.add, ALU.subtract), h0, free_tmp[i])
            h1 = act(lambda e: e.activation(d[1], tm, ACT.Copy), r, pack_last)
            free_tmp[i] = part_done[b, c] = pool(lambda e: e.tensor_tensor(d[2], tm, d[1], ALU.subtract), h1, pack_last)
        return rest

    def values(b, j, half):
        src, q = hT[n_hT % 2], n_hT % 2
        s, bk = slot()
        for i in range(2):
            for cc in range(2):
                m = pe(lambda e, cc=cc, i=i: e.matmul(bk[:, i * D:i * D + D], src[:, cc, (2 * half + i) * 128:(2 * half + i) * 128 + 128],
                                                      wt["v"][:, cc, :], start=cc == 0, stop=cc == 1), hTw[b, "v", j], freed[s])
        free_hT[q] = m

        def rest():
            for i in range(2):
                t = dve(lambda e, i=i: e.tensor_tensor(
                    v[b % 2][:, 4 * j + 2 * half + i, :, 0:DA], bk[:, i * D:i * D + D].rearrange("p (h d) -> p h d", d=DA),
                    brow["v"][:, :].rearrange("p (h d) -> p h d", d=DA), ALU.add), m, pv_last.get(b - 2))
            freed[s] = v_done[b] = t
        return rest

    def out_T(b, w0):
        nonlocal n_hT, at_read
        n_hT += w0 % 4 == 0
        dst = hT[n_hT % 2]
        s, bk = slot()
        for i in range(2):
            for c in range(2):
                m = pe(lambda e, i=i, c=c: e.transpose(bk[:, c * 256 + i * 128:c * 256 + i * 128 + 128], at[:, w0 + i, c * 128:c * 128 + 128],
                                                       ident[:, :]), norm_last, freed[s])
        at_read = m
        o = (w0 % 4) * 128
        aTw[b, w0] = freed[s] = act(lambda e: e.activation(dst[:, :, o:o + 256], bk.rearrange("p (c n) -> p c n", c=2), ACT.Copy),
                                    m, free_hT[n_hT % 2])

    def out_project(b, w0):
        q = n_hT % 2
        src = hT[q]
        s, bk = slot()
        for i in range(2):
            for c in range(2):
                o = ((w0 + i) % 4) * 128
                m = pe(lambda e, i=i, c=c, o=o: e.matmul(bk[:, i * D:i * D + D], src[:, c, o:o + 128], wt["o"][:, c, :],
                                                         start=c == 0, stop=c == 1), aTw[b, w0], freed[s])
        free_hT[q] = m
        k = where[b, "o", w0 // 4]
        i0 = w0 % 4
        x2 = xc[k % 2][:, i0:i0 + 2, :]

        def rest():
            t = freed[s] = dve(lambda e: e.tensor_tensor(x2, bk.rearrange("p (w d) -> p w d", d=D), x2, ALU.add), m, loaded[k])
            t = x1s = dve(lambda e: e.tensor_tensor(x2, x2, brow["o"][:, :].unsqueeze(1).to_broadcast([128, 2, D]), ALU.add), t)
            for i in range(2):
                t = dve(lambda e, i=i: e.bn_stats(st[:, i, :], xc[k % 2][:, i0 + i, :]), x1s)
            for i in range(2):
                t = dve(lambda e, i=i: e.bn_aggr(mv2[:, i0 + i, :], st[:, i, :]), t, mv2_read)
            t = dve(lambda e: e.tensor_scalar(ve[:, 0:2], mv2[:, i0:i0 + 2, 1], EPS, None, ALU.add), t)
            t = pool(lambda e: e.tensor_tensor(rs2[:, i0:i0 + 2], ve[:, 0:2], nh[:, 0:2], ALU.pow), t, c_nh)
            if i0 == 2:
                x1_done[b] = sp.dma(cs[k % 2], lambda e: e.dma_start(
                    x1[b, (w0 - 2) * 128:(w0 + 2) * 128, :].rearrange("(w p) d -> p w d", p=128), xc[k % 2][:, :, :]), x1s)
            seconds.append((b, w0, k, i0, t))
        return rest

    def second():
        nonlocal mv2_read
        if seconds:
            b, w0, k, i0, t = seconds.pop()
            for i in range(2):
                mv2_read = dve(lambda e, i=i: e.tensor_scalar(xs[:, b * W + w0 + i, :], xc[k % 2][:, i0 + i, :], mv2[:, i0 + i, 0:1],
                                                              rs2[:, i0 + i:i0 + i + 1], ALU.subtract, ALU.mult), t, at_read)
            if i0 == 2:
                released[k] = [x1_done[b], mv2_read]
                load(k + 2)

    def pack(g):
        nonlocal pack_last
        b, h = divmod(g, HA)
        s, r0 = g % 3, 16 * (h % 8)
        for n, dst, order in (("q", qp[s], QPART), ("k", kp[s], KPART)):
            for j, p in enumerate(order):
                pack_last = pack_of[g] = sp.dma(cp[s], lambda e, n=n, dst=dst, j=j, p=p: e.dma_start(
                    dst[16 * j:16 * j + 16, :], parts[n][r0:r0 + 16, p, :]), part_done[b, h // 8], qk_read.get(s))

    p1_last = {}

    def pass1(g, qb, c):
        nonlocal junk_w
        s, i = g % 3, c % 2
        m = pe(lambda e: e.matmul(bank[i][:, :], qp[s][0:96, qb * 128:qb * 128 + 128], kp[s][0:96, c * 512:c * 512 + 512],
                                  start=True, stop=True), pack_of[g], free_bank[i])
        o = 512 * c - 128 * qb
        if -512 - BAND < o < 128 + BAND:
            r = junk_w = dve(lambda e: e.tensor_tensor_reduce(junk[:, :], bank[i][:, :], gw[:, o + WIDE0:o + WIDE0 + 512], 1.0, 0.0,
                                                              ALU.add, ALU.max, mx[g % 2][:, qb, c:c + 1]),
                             m, c_gw, free_mx[g % 2], junk_w)
        else:
            r = dve(lambda e: e.tensor_reduce(mx[g % 2][:, qb, c:c + 1], bank[i][:, :], X, ALU.max), m, free_mx[g % 2])
        free_bank[i] = p1_last[g] = r

    def rows(g):
        nonlocal pk_done
        t = free_mx[g % 2] = dve(lambda e: e.tensor_reduce(nm[:, :], mx[g % 2][:, :, :], X, ALU.max, negate=True), p1_last[g])
        t = dve(lambda e: e.tensor_copy(pk[:, 0, :], nm[:, :]), t, free_pk)
        t = dve(lambda e: e.tensor_tensor(r1[:, :], nm[:, :], pk[:, 0, :], ALU.subtract), t)
        t = dve(lambda e: e.tensor_copy(pk[:, 1, :], r1[:, :]), t)
        pk_done = dve(lambda e: e.tensor_tensor(pk[:, 2, :], r1[:, :], pk[:, 1, :], ALU.subtract), t)

    def rows_T(g):
        nonlocal free_row, free_pk
        s = g % 3
        ptb = pt[:, :].bitcast(BF16)
        t = free_pk = pe(lambda e: e.transpose(ptb[0:48, 0:128], pk[:, :, :].rearrange("p a b -> p (a b)"), identb[:, :]), pk_done, idb, freed[0])
        t = freed[0] = dve(lambda e: e.tensor_copy(row[:, :], ptb[0:48, 0:128]), t, free_row)
        for p in range(3):
            free_row = row_of[g] = sp.dma(cr[s], lambda e, p=p: e.dma_start(qp[s][96 + p:97 + p, :], row[16 * p:16 * p + 16, :]),
                                          t, qk_read.get(s))

    exps = {}

    def pass2(g, kb, u):
        s = g % 3
        n = (g * W + kb) * 2 + u
        for c in range(2):
            m = pe(lambda e, c=c: e.matmul(wide[u][:, c * 512:c * 512 + 512], kp[s][0:99, kb * 128:kb * 128 + 128],
                                           qp[s][0:99, u * 1024 + c * 512:u * 1024 + c * 512 + 512],
                                           start=True, stop=True, skip_group_check=True), pack_of[g], row_of[g], c_one, free_wide[u])
        qk_read[s] = m
        for q in range(4):
            for bk, c0, p0, n_ in windows(kb * 128 + 32 * q):
                if bk // 2 == u:
                    o = wide[u][:, bk % 2 * 512:bk % 2 * 512 + 512]
                    m = pe(lambda e, q=q, c0=c0, p0=p0, n_=n_, o=o: e.matmul(
                        o[32 * q:32 * q + 32, c0:c0 + n_], sel[:, :], mt[:, p0:p0 + n_], start=False, stop=True, skip_group_check=True),
                        c_mt, c_sel)
        free_wide[u] = exps[n] = act(lambda e: e.activation(pr[n % NP][:, :], wide[u][:, :], ACT.Exp, scale=0.25), m, free_pr[n % NP])

    def pv(g, kb, js):
        b, h = divmod(g, HA)
        n = (g * W + kb) * 2
        for j in js:
            i = (n + j // 2) % NP
            m = free_pr[i] = pe(lambda e, j=j, i=i: e.matmul(
                po[32 * j:32 * j + DA + 1, :], v[b % 2][:, kb, h, :], pr[i][:, (j % 2) * 512:(j % 2) * 512 + 512],
                start=kb == 0, stop=kb == W - 1, skip_group_check=True),
                exps[n + j // 2], free_po if kb == 0 else None, v_done[b], c_v1)
        pv_last[b] = m

    def finish(g):
        nonlocal free_po, osb_done
        osb_done = free_po = act(lambda e: e.activation(osb[:, :], po[:, :], ACT.Copy), pv_last[g // HA], free_osb)

    def finish_T(g):
        nonlocal free_osb, norm_last
        h = g % HA
        for s in range(4):
            t = free_osb = pe(lambda e, s=s: e.transpose(pt[:, s * 128:s * 128 + 128], osb[:, s * 128:s * 128 + 128], ident[:, :]),
                              osb_done, freed[0])
        z = pt[:, :].rearrange("p (s j e) -> p s j e", s=4, j=4)
        r = dve(lambda e: e.reciprocal(rc[:, :, :], z[:, :, :, DA]), t)
        norm_last = freed[0] = dve(lambda e: e.tensor_tensor(
            at[:, :, h * DA:h * DA + DA].rearrange("p (j s) d -> p s j d", s=4), z[:, :, :, 0:DA],
            rc[:, :, :].unsqueeze(3).to_broadcast([128, 4, 4, DA]), ALU.mult), r, at_read)

    for j in range(4):
        stats(0, j)
        for half in range(2):
            normal(0, "v", j, half)
            turned(0, "v", j, half)
        for r in [values(0, j, half) for half in range(2)]:
            r()
    for j in range(4):
        for half in range(2):
            normal(0, 0, j, half)
            turned(0, 0, j, half)
        for r in [project(0, 0, j, n) for n in "qk"]:
            r()
    pack(0)
    pack(1)
    constants()

    units, before = {}, {}

    def plan(n, f, *args):
        while n in units or f in (project, values, out_project) and n % W in (1, W - 2):
            n += 1
        units[n] = lambda: f(*args)
        if f is turned:
            before[n - 1] = lambda: normal(*args)
        return n

    S = HA * W
    for b in range(NB):
        n0 = b * S
        if b:
            n = n0 + 2
            for w0 in range(0, W, 2):
                n = plan(n, out_T, b - 1, w0)
                n = plan(n, out_project, b - 1, w0)
        n = n0 + 85
        for j in range(4):
            for f in ((turned, b, 1, j, 0), (turned, b, 1, j, 1), (project, b, 1, j, "q"), (project, b, 1, j, "k")):
                n = plan(n, *f)
        assert n <= n0 + 101
        if b + 1 < NB:
            n = n0 + 114
            for j in range(4):
                n = plan(n, stats, b + 1, j) + 2
                for f in ((turned, b + 1, "v", j, 0), (turned, b + 1, "v", j, 1), (values, b + 1, j, 0), (values, b + 1, j, 1)):
                    n = plan(n + 1, *f)
            n = n0 + 213
            for j in range(4):
                for f in ((turned, b + 1, 0, j, 0), (turned, b + 1, 0, j, 1), (project, b + 1, 0, j, "q"), (project, b + 1, 0, j, "k")):
                    n = plan(n, *f)
            assert n <= n0 + 229
    packs = {16 * (g - 2) + (7 if g % 8 == 0 else 1): g for g in range(2, NB * HA)}

    free_bank[0], free_bank[1] = freed[1], freed[2]
    free_wide[0], free_wide[1] = freed[3:5], freed[5:7]
    scratch_n = 1
    after, seconds = [], []
    later = []
    i1 = 0

    def p1_unit(c):
        nonlocal i1
        if i1 < NB * S:
            g, qb = divmod(i1, W)
            pass1(g, qb, c)
            if c == 3:
                i1 += 1
                if qb == W - 1:
                    rows(g)
                    later.append(lambda: rows_T(g))

    LEAD = W + 2
    for n in range(-LEAD, NB * S + 1):
        if n in packs:
            pack(packs[n])
        todo = list(later)
        later.clear()
        g, kb = divmod(n, W)
        p1_unit(0)
        if 0 <= n < NB * S:
            pass2(g, kb, 0)
        p1_unit(1)
        second()
        if after:
            after.pop()()
        if n in before:
            before[n]()
        if n > 0:
            pv(*divmod(n - 1, W), (0, 1))
        if n in units and (rest := units[n]()):
            after.append(rest)
        p1_unit(2)
        if 0 <= n < NB * S:
            pass2(g, kb, 1)
        p1_unit(3)
        if n > 0:
            pv(*divmod(n - 1, W), (2, 3))
            if kb == 0:
                finish(g - 1)
                later.append(lambda g=g: finish_T(g - 1))
        for f in todo:
            f()
    for f in later:
        f()

    freed = [freed[0], free_bank[0], free_bank[1], free_wide[0], free_wide[0], free_wide[1], free_wide[1]]
    scratch_n = 7
    for w0 in range(0, W, 2):
        out_T(NB - 1, w0)
        second()
        out_project(NB - 1, w0)()
    second()
    sp(None, list(x1_done.values()))
    ph.run()


HL, DL = 8, 64
NEG = -3.3895313892515355e38
FC, FW = 6, 114
ROUNDS = [(0, 112), (112, 15)]


def split(ph, hi, lo, x, free=(), *waits, scale=None):
    if scale is None:
        h = ph.act(lambda e: e.activation(hi, x, ACT.Copy), free, *waits)
        return ph.dve(lambda e: e.tensor_tensor(lo, x, hi.bitcast(F32), ALU.subtract), h, free, *waits)
    h = ph.act(lambda e: e.activation(hi, x, ACT.Copy, scale=scale), free, *waits)
    return ph.dve(lambda e: e.scalar_tensor_tensor(lo, x, scale, hi.bitcast(F32), ALU.mult, ALU.subtract), h, free, *waits)


PASSES = ((0, 0), (0, 1), (1, 0))


def shift(ph, xs, dst, counter, g, waits):
    t = 4 * g
    up, z = xs[:, t:t + 4, 128:256], None
    for p, n in ROUNDS:
        ph.sp.dma(counter, lambda e, p=p, n=n: e.dma_start(dst[p + 1:p + 1 + n, :, :], up[p:p + n, :, :]), waits)
    first = t % W == 0
    if first:
        z = ph.pool(lambda e: e.memset(dst[0:1, 0, :], 0.0), waits)
    o = int(first)
    return [z, ph.sp.dma(counter, lambda e: e.dma_start(dst[0:1, o:4, :], xs[127:128, t - 1 + o:t + 3, 128:256]), waits)]


def shift_read(shifted, t):
    return [shifted[t // 4], shifted[(t + 1) // 4] if (t + 1) % W else None]


def rotary():
    half = np.arange(0, DL, 2, dtype=np.float32)
    inv = np.float32(1.0) / np.float32(10000.0) ** (half / np.float32(DL))
    t = np.arange(L, dtype=np.float32)
    f = t[:, None] * inv[None, :]
    f = np.concatenate([f, f], 1)
    base = (half + np.float32(0.4 * DL)) / np.float32(1.4 * DL)
    power = (t - np.float32(L // 2)) / np.float32(64.0)
    s = base[None, :] ** power[:, None]
    s = np.concatenate([s, s], 1)
    sign = np.concatenate([-np.ones(32), np.ones(32)]).astype(np.float32)
    cos, sin = np.cos(f), np.sin(f) * sign
    e = np.float32(8.0)
    q, k = np.stack([cos * s * e, sin * s * e], 1), np.stack([cos / s, sin / s], 1)
    return np.ascontiguousarray(np.stack([q, k], 1).astype(np.float32).reshape(W, 128, 2, 2, DL).transpose(1, 0, 2, 3, 4))


def causal():
    r, c = np.arange(128)[:, None], np.arange(128)[None, :]
    m = np.concatenate([np.where(c >= r, 0.0, NEG), np.where(c <= r, 0.0, NEG)], 1)
    return np.concatenate([m, m], 1).astype(np.float32)


def local_layer(nc, xs, layer, a):
    ph = Phase(nc, f"l{layer}")
    pe, act, dve, pool, sp = ph.pe, ph.act, ph.dve, ph.pool, ph.sp
    sb = ph.sb
    wq = [sb(f"wqkv{i}", [128, 2, 3 * HL * DL], F32R) for i in range(2)]
    wo = [sb(f"wo{i}", [128, 4, D], F32R) for i in range(2)]
    tab = sb("tab", [128, W, 2, 2, DL])
    qsc = sb("qsc", [128, 2, 2, DL])
    ident, identb = sb("ident", [128, 128]), sb("identb", [128, 128], BF16)
    mask = sb("mask", [128, 512], BF16)
    nh = sb("nh", [128, 16])
    sh = [sb(f"sh{i}", [128, 4, 128]) for i in range(2)]
    hT = [[sb(f"hT{i}{k}", [128, 256], F32R) for k in range(2)] for i in range(2)]
    qk = [sb(f"qk{i}", [128, 2, HL, DL]) for i in range(2)]
    sq = sb("sq", [128, 2, HL, DL])
    t1 = [sb(f"t1{i}", [128, 2, HL, DL]) for i in range(2)]
    t2 = sb("t2", [128, 2, HL, DL])
    ss, ri = [sb(f"ss{i}", [128, 16]) for i in range(2)], [sb(f"ri{i}", [128, 16]) for i in range(2)]
    qT = [sb(f"qT{i}", [128, 4, 128]) for i in range(2)]
    kT = [sb(f"kT{i}", [128, 4, 2, 128]) for i in range(3)]
    v = [sb(f"v{i}", [128, HL * DL]) for i in range(5)]
    p = [sb(f"p{i}", [128, HL, 2, 128]) for i in range(2)]
    nm, sm, rc = ([sb(f"{n}{i}", [128, HL]) for i in range(2)] for n in ("nm", "sm", "rc"))
    pT = [sb(f"pT{i}", [128, 2, 2, 128]) for i in range(4)]
    oT = [[sb(f"oT{i}{k}", [128, 512], F32R) for k in range(2)] for i in range(2)]
    G = [ph.ps(f"G{i}", [128, 512]) for i in range(2)]
    T = ph.ps("T", [128, 512])
    S = [ph.ps(f"S{i}", [128, 512]) for i in range(2)]
    R = [ph.ps(f"R{i}", [128, 512]) for i in range(2)]
    O = ph.ps("O", [128, 512])

    ci, cq, cw = ph.counter("ci"), [ph.counter(f"cq{i}") for i in range(2)], ph.counter("cw")
    c_ident = sp.dma(ci, lambda e: e.dma_start(ident[:, :], a["ident"]))
    csh = [ph.counter(f"sh{i}") for i in range(2)]
    shifted, sh_read = {}, {}
    shifted[0] = shift(ph, xs, sh[0], csh[0], 0, None)
    stage, c_wq = [x[:, :, :, :].rearrange("p a h d -> p a (h d)") for x in (t1[0], t2)], {}
    for n in range(3):
        c = sp.dma(cq[n % 2], lambda e, n=n: e.dma_start(stage[n % 2], a["wqkv"][layer, :, n * 512:n * 512 + 512].rearrange("(c p) n -> p c n", p=128)),
                   c_wq.get(n - 2))
        c_wq[n] = split(ph, wq[0][:, :, n * 512:n * 512 + 512], wq[1][:, :, n * 512:n * 512 + 512], stage[n % 2], None, c)
    sp.dma(cw, lambda e: e.dma_start(tab[:, :, :, :, :], a["rotary"]))
    sp.dma(cw, lambda e: e.dma_start(qsc[:, :, :, :].rearrange("p a b d -> p (a b d)"), a["qsc"][layer].partition_broadcast(128)))
    mask32, wraw = sq[:, 0, :, :].rearrange("p h d -> p (h d)"), t1[1][:, :, :, :].rearrange("p a h d -> p (a h d)")
    sp.dma(cw, lambda e: e.dma_start(mask32, a["causal"]))
    const = sp.dma(cw, lambda e: e.dma_start(wraw.rearrange("p (c n) -> p c n", n=D), a["lwo"][layer].rearrange("(c p) n -> p c n", p=128)))
    c_nh = pool(lambda e: e.memset(nh[:, :], -0.5))
    c_kT = [pool(lambda e, i=i: e.memset(kT[i][:, :, :, :], 0.0)) for i in range(3)]
    idb = dve(lambda e: e.tensor_copy(identb[:, :], ident[:, :]), c_ident)

    def late():
        nonlocal c_mask, c_tab, c_wo
        c_tab = [dve(lambda e, i=i: e.tensor_tensor(tab[:, :, i, :, :], tab[:, :, i, :, :],
                                                    qsc[:, i, :, :].unsqueeze(1).to_broadcast([128, W, 2, DL]), ALU.mult), const)
                 for i in range(2)]
        c_mask = dve(lambda e: e.tensor_copy(mask[:, :], mask32), const)
        wide = [x[:, :, :].rearrange("p a n -> p (a n)") for x in wo]
        c_wo = split(ph, wide[0], wide[1], wraw, None, const)

    c_mask = c_tab = c_wo = None
    free_G, free_T, free_S, free_R, free_O = [None] * 2, [None], [None] * 2, [None] * 2, [None]
    xT, hTr, qkE, qkR, t1w, t1r, ready = {}, {}, {}, {}, {}, {}, {}
    qTw, qTr, kTw, kTr, vw, vr = {}, {}, {}, {}, {}, {}
    pw, pn, pr, recip, pTr, ow, owr, mxs, tsum = {}, {}, {}, {}, {}, {}, {}, {}, {}
    squares, products, inverse, rotated = {}, {}, {}, {}
    t2r, sqr, done = [None], [None], {}

    def x_T(t):
        g = t // 4
        src = [xs[:, t, 0:128], sh[g % 2][:, t % 4, :]]
        for c in range(2):
            m = pe(lambda e, c=c: e.transpose(G[0][:, c * 128:c * 128 + 128], src[c], ident[:, :]), c_ident, shifted[g], free_G[0])
        sh_read[g] = m
        xT[t] = free_G[0] = split(ph, hT[t % 2][0][:, :], hT[t % 2][1][:, :], G[0][:, 0:256], hTr.get(t - 2), m)

    def qkv(t, n):
        g = G[n % 2]
        i = 0
        for x, z in PASSES:
            for c in range(2):
                m = pe(lambda e, c=c, x=x, z=z, i=i: e.matmul(g[:, :], hT[t % 2][x][:, c * 128:c * 128 + 128], wq[z][:, c, n * 512:n * 512 + 512],
                                                              start=i == 0, stop=i == 5), xT[t], c_wq[n], free_G[n % 2])
                i += 1
        hTr[t] = m
        if n < 2:
            free_G[n] = qkE[t, n] = act(lambda e: e.activation(qk[t % 2][:, n, :, :].rearrange("p h d -> p (h d)"), g[:, :], ACT.Copy),
                                        m, qkR.get(t - 2))
        else:
            free_G[0] = vw[t] = act(lambda e: e.activation(v[t % 5][:, :], g[:, :], ACT.Copy), m, vr.get(t - 5))

    def rotate(t):
        s = t % 2
        src, w = qk[s], t % W
        squares[t] = act(lambda e: e.activation(sq[:, :, :, :], src[:, :, :, :], ACT.Square),
                         qkE[t, 0], qkE[t, 1], sqr[0], c_mask)
        a1 = dve(lambda e: e.tensor_tensor(t1[s][:, :, :, :], src[:, :, :, :],
                                           tab[:, w, :, 0, :].unsqueeze(2).to_broadcast([128, 2, HL, DL]), ALU.mult),
                 qkE[t, 0], qkE[t, 1], c_tab, c_wo, c_wq[0], t1r.get(t - 2))
        for i in range(2):
            a2 = dve(lambda e, i=i: e.tensor_tensor(
                t2[:, :, :, 32 * i:32 * i + 32], src[:, :, :, 32 - 32 * i:64 - 32 * i],
                tab[:, w, :, 1, 32 * i:32 * i + 32].unsqueeze(2).to_broadcast([128, 2, HL, 32]), ALU.mult), t2r[0], c_wq[1])
        qkR[t] = [squares[t], a2]
        products[t] = [a1, a2]

    def lengths(t):
        s = t % 2
        sqr[0] = r = dve(lambda e: e.tensor_reduce(ss[s][:, :], sq[:, :, :, :].rearrange("p a h d -> p (a h) d"), X, ALU.add),
                         squares[t], t1r.get(t - 2))
        r = dve(lambda e: e.tensor_scalar(ss[s][:, :], ss[s][:, :], 1e-24, None, ALU.max), r)
        r = pool(lambda e: e.tensor_tensor(ri[s][:, :], ss[s][:, :], nh[:, :], ALU.pow), r, c_nh)
        inverse[t] = r
        t2r[0] = rotated[t] = pool(lambda e: e.tensor_tensor(t1[s][:, :, :, :], t1[s][:, :, :, :], t2[:, :, :, :], ALU.add), products[t])

    def scale(t):
        s = t % 2
        flat_ = t1[s][:, :, :, :].rearrange("p a h d -> p (a h) d")
        ready[t] = dve(lambda e: e.tensor_tensor(flat_, flat_, ri[s][:, :].unsqueeze(2).to_broadcast([128, 16, DL]), ALU.mult), rotated[t], inverse[t])

    def qk_T(t, n):
        for i in range(4):
            m = pe(lambda e, i=i: e.transpose(T[:, i * 128:i * 128 + 128],
                                              t1[t % 2][:, n, 2 * i:2 * i + 2, :].rearrange("p h d -> p (h d)"), ident[:, :]),
                   ready[t], free_T[0])
        t1r[t] = m
        if n == 0:
            free_T[0] = qTw[t] = act(lambda e: e.activation(qT[t % 2][:, :, :].rearrange("p a n -> p (a n)"), T[:, :], ACT.Copy), m, qTr.get(t - 2))
        else:
            for i in range(2):
                z = dve(lambda e, i=i: e.tensor_copy(kT[t % 3][64 * i:64 * i + 64, :, i, :],
                                                     T[64 * i:64 * i + 64, :].rearrange("p (a n) -> p a n", a=4)),
                        m, c_kT, kTr.get(t - 3), kTr.get(t - 2))
            free_T[0] = kTw[t] = z

    def sim(t, pair):
        w, s = t % W, S[pair % 2]
        z = s[:, :].rearrange("p (h k n) -> p h k n", h=2, k=2)
        pe(lambda e: e.matmul(s[:, :], identb[:, :], mask[:, :], start=True, stop=False, skip_group_check=True),
           idb, c_mask, free_S[pair % 2])
        for k in ([0, 1] if w else [1]):
            m = pe(lambda e, k=k: e.matmul(z[:, :, k, :], qT[t % 2][:, pair, :], kT[(t - 1 + k) % 3][:, pair, :, :],
                                           start=False, stop=True, skip_group_check=True), qTw[t], kTw[t])
        qTr[t] = kTr[t] = m
        x = dve(lambda e: e.tensor_reduce(nm[t % 2][:, 2 * pair:2 * pair + 2], s[:, :].rearrange("p (h k) -> p h k", h=2) if w else z[:, :, 1, :],
                                          X, ALU.max, negate=True), m, pw.get((t - 2, pair)))
        for h in range(2):
            hh = 2 * pair + h
            dst = p[t % 2][:, hh, :, :].rearrange("p k n -> p (k n)") if w else p[t % 2][:, hh, 1, :]
            src = s[:, h * 256:h * 256 + 256] if w else z[:, h, 1, :]
            y = act(lambda e, hh=hh, dst=dst, src=src: e.activation(dst, src, ACT.Exp, bias=nm[t % 2][:, hh:hh + 1],
                                                                    accum_out=sm[t % 2][:, hh:hh + 1]),
                    x, pr.get((t - 2, pair)), recip.get((t - 2, pair)))
        free_S[pair % 2] = pw[t, pair] = y

    def normalise(t, pair):
        w, o = t % W, 2 * pair
        recip[t, pair] = r = dve(lambda e: e.reciprocal(rc[t % 2][:, o:o + 2], sm[t % 2][:, o:o + 2]), pw[t, pair], pn.get((t - 2, pair)))
        z = p[t % 2][:, o:o + 2, :, :]
        z = z.rearrange("p h k n -> p h (k n)") if w else z[:, :, 1, :]
        pn[t, pair] = pool(lambda e: e.tensor_tensor(z, z, rc[t % 2][:, o:o + 2].unsqueeze(2).to_broadcast([128, 2, 256 if w else 128]),
                                                     ALU.mult), r)

    def p_T(t, pair):
        w, r = t % W, R[pair % 2]
        ks = [0, 1] if w else [1]
        for h in range(2):
            for k in ks:
                m = pe(lambda e, h=h, k=k: e.transpose(r[:, (2 * k + h) * 128:(2 * k + h) * 128 + 128], p[t % 2][:, 2 * pair + h, k, :], ident[:, :]),
                       pn[t, pair], free_R[pair % 2])
        pr[t, pair] = m
        dst = pT[pair][:, :, :, :].rearrange("p k h n -> p (k h n)")
        lo = 0 if w else 256
        if pair % 2:
            free_R[1] = y = dve(lambda e: e.tensor_copy(dst[:, lo:512], r[:, lo:512]), m, pTr.get(pair))
        else:
            free_R[0] = y = act(lambda e: e.activation(dst[:, lo:512], r[:, lo:512], ACT.Copy), m, pTr.get(pair))
        ks = ks
        pw[t, pair, "T"] = y

    def pv(t, pair):
        w = t % W
        for k in ([0, 1] if w else [1]):
            for h in range(2):
                hh = 2 * pair + h
                m = pe(lambda e, h=h, k=k, hh=hh: e.matmul(
                    O[64 * h:64 * h + 64, pair * 128:pair * 128 + 128], v[(t - 1 + k) % 5][:, hh * DL:hh * DL + DL], pT[pair][:, k, h, :],
                    start=k == 0 or w == 0, stop=k == 1, skip_group_check=True), pw[t, pair, "T"], vw[t], free_O[0])
        pTr[pair] = vr[t - 1] = m
        if pair == 3:
            free_O[0] = ow[t] = split(ph, oT[t % 2][0][:, :], oT[t % 2][1][:, :], O[:, :], owr.get(t - 2), m)

    def out(t):
        i = 0
        for x, z in PASSES:
            for c in range(4):
                m = pe(lambda e, c=c, x=x, z=z, i=i: e.matmul(G[1][:, 0:D], oT[t % 2][x][:, c * 128:c * 128 + 128], wo[z][:, c, :],
                                                              start=i == 0, stop=i == 11), ow[t], c_wo, free_G[1])
                i += 1
        owr[t] = m
        done[t] = free_G[1] = dve(lambda e: e.tensor_tensor(xs[:, t, :], G[1][:, 0:D], xs[:, t, :], ALU.add), m, shift_read(shifted, t))

    def on(f, t, *args):
        if 0 <= t < NT:
            f(t, *args)

    on(x_T, 0)
    for n in range(NT + 4):
        on(sim, n - 2, 0)
        on(scale, n - 1)
        on(qkv, n, 0)
        on(sim, n - 2, 1)
        on(normalise, n - 2, 0)
        on(p_T, n - 3, 0)
        on(qkv, n, 1)
        on(qk_T, n - 1, 0)
        if n == 0:
            late()
        on(rotate, n)
        on(normalise, n - 2, 1)
        on(p_T, n - 3, 1)
        on(sim, n - 2, 2)
        on(qkv, n, 2)
        on(pv, n - 3, 0)
        on(lengths, n)
        on(qk_T, n - 1, 1)
        on(p_T, n - 3, 2)
        on(pv, n - 3, 1)
        on(p_T, n - 3, 3)
        on(sim, n - 2, 3)
        on(normalise, n - 2, 2)
        g = (n + 4) // 4
        if n % 4 == 0 and g < NT // 4:
            shifted[g] = shift(ph, xs, sh[g % 2], csh[g % 2], g, sh_read.get(g - 2))
        on(x_T, n + 1)
        on(normalise, n - 2, 3)
        on(pv, n - 3, 2)
        on(out, n - 4)
        on(pv, n - 3, 3)
    ph.run()


def feed_forward(nc, xs, layer, last, x1, y, a):
    ph = Phase(nc, f"f{layer}")
    pe, act, dve, pool, sp = ph.pe, ph.act, ph.dve, ph.pool, ph.sp
    sb = ph.sb
    NG = NT // 4
    w1, w2 = [sb(f"w1{i}", [128, 2, 2 * FC * FW], F32R) for i in range(2)], [sb(f"w2{i}", [FW, FC, D], F32R) for i in range(2)]
    r1, r2 = sb("r1", [128, 2, 2 * FC * FW]), sb("r2", [FW, FC, D])
    b1 = sb("b1", [FW, 2 * FC])
    lg, lb = sb("lg", [128, 2]), sb("lb", [128, 2])
    b2 = sb("b2", [128, D])
    ident = sb("ident", [128, 128])
    nh = sb("nh", [128, 4])
    sh = [sb(f"sh{i}", [128, 4, 128]) for i in range(3)]
    st = sb("st", [128, 2, 6])
    mv, ve, rs = ([sb(f"{n}{i}", [128, 4, w]) for i in range(2)] for n, w in (("mv", 2), ("ve", 1), ("rs", 1)))
    hn = [sb(f"hn{i}", [128, D]) for i in range(4)]
    hT = [[sb(f"hT{i}{k}", [128, 2, 512], F32R) for k in range(2)] for i in range(2)]
    gg = [sb(f"gg{i}", [FW, 512]) for i in range(2)]
    uf = [sb(f"uf{i}", [FW, 512]) for i in range(2)]
    NU = 9
    u = [[sb(f"u{i}_{k}", [FW, 512], F32R) for k in range(2)] for i in range(NU)]
    xo = [sb(f"xo{i}", [128, 4, D]) for i in range(2)] if last else None
    T = [ph.ps(f"T{i}", [128, 512]) for i in range(2)]
    F = [ph.ps(f"F{i}", [128, 512]) for i in range(4)]
    Y = [ph.ps(f"Y{i}", [128, 512]) for i in range(2)]

    c_nh = pool(lambda e: e.memset(nh[:, :], -0.5))
    csh = [ph.counter(f"sh{i}") for i in range(3)]
    cx, cy = [ph.counter(f"x{i}") for i in range(2)], ph.counter("y")
    shifted, sh_read = {}, {}
    shifted[0] = shift(ph, xs, sh[0], csh[0], 0, None)
    cs, c1, cw = ph.counter("cs"), ph.counter("c1"), ph.counter("cw")
    c_ident = sp.dma(cs, lambda e: e.dma_start(ident[:, :], a["ident"]))
    for d, n in ((b1, "b1"), (lg, "lg"), (lb, "lb")):
        sp.dma(c1, lambda e, d=d, n=n: e.dma_start(d[:, :], a[n][layer]))
    c_r1 = sp.dma(c1, lambda e: e.dma_start(r1[:, :, :], a["w1"][layer].rearrange("(c p) n -> p c n", p=128)))
    for g in range(1, min(3, NG)):
        shifted[g] = shift(ph, xs, sh[g], csh[g], g, None)
    sp.dma(cw, lambda e: e.dma_start(b2[:, :], a["b2"][layer].partition_broadcast(128)))
    c_r2 = sp.dma(cw, lambda e: e.dma_start(r2[:, :, :], a["w2"][layer].rearrange("(c p) n -> p c n", p=FW)))

    free_T, free_F, free_Y = [None] * 2, [None] * 4, [None] * 2
    free_hn, hTw, hTr, uw, ur, free_gg, free_uf, stats, normed, mv_read = [None] * 4, {}, {}, {}, {}, [None] * 2, [None] * 2, {}, {}, {}
    xin, xor_, done = {}, {}, {}

    def statistics(g, i):
        s, t = g % 2, 4 * g + i
        prev = mv_read.get(g - 2)
        dve(lambda e: e.bn_stats(st[:, 0, :], xs[:, t, 0:128]), stats.get("st"))
        x = dve(lambda e: e.bn_stats(st[:, 1, :], sh[g % 3][:, i, :]), shifted[g], stats.get("st"))
        x = stats["st"] = dve(lambda e: e.bn_aggr(mv[s][:, i, :], st[:, :, :].rearrange("p a b -> p (a b)")), x, prev)
        if i == 3:
            x = dve(lambda e: e.tensor_scalar(ve[s][:, :, 0], mv[s][:, :, 1], EPS, None, ALU.add), x, stats.get(g - 2))
            stats[g] = pool(lambda e: e.tensor_tensor(rs[s][:, :, 0], ve[s][:, :, 0], nh[:, :], ALU.pow), x, c_nh, prev)

    def normal(g, i):
        s, t = g % 2, 4 * g + i
        for c, src in enumerate((xs[:, t, 0:128], sh[g % 3][:, i, :])):
            n = dve(lambda e, c=c, src=src: e.tensor_scalar(hn[i][:, c * 128:c * 128 + 128], src, mv[s][:, i, 0:1], rs[s][:, i, :],
                                                            ALU.subtract, ALU.mult), stats[g], free_hn[i])
        sh_read[g] = mv_read[g] = normed[g, i] = n

    def turned(g, i):
        for c in range(2):
            m = pe(lambda e, c=c: e.transpose(T[c][:, i * 128:i * 128 + 128], hn[i][:, c * 128:c * 128 + 128], ident[:, :]),
                   normed[g, i], c_ident, free_T[c] if i == 0 else None)
        free_hn[i] = m
        if i == 3:
            for c in range(2):
                free_T[c] = hTw[g] = split(ph, hT[g % 2][0][:, c, :], hT[g % 2][1][:, c, :], T[c][:, :], hTr.get(g - 2), m)

    def hidden(g, j):
        fa, fg = F[2 * (j % 2)], F[2 * (j % 2) + 1]
        for f, k, o in ((fg, FC + j, 1), (fa, j, 0)):
            n = 0
            for x, z in PASSES:
                for c in range(2):
                    m = pe(lambda e, c=c, f=f, k=k, x=x, z=z, n=n: e.matmul(
                        f[0:FW, :], w1[x][:, c, k * FW:k * FW + FW], hT[g % 2][z][:, c, :], start=n == 0, stop=n == 5),
                        hTw[g], c_w1, free_F[2 * (j % 2) + o])
                    n += 1
            if o:
                mg = m
        hTr[g] = m
        x = free_F[2 * (j % 2) + 1] = act(lambda e: e.activation(gg[j % 2][:, :], fg[0:FW, :], ACT.Gelu, bias=b1[:, FC + j:FC + j + 1]),
                                          mg, c_b1, free_gg[j % 2])
        x = dve(lambda e: e.scalar_tensor_tensor(uf[j % 2][:, :], fa[0:FW, :], b1[:, j:j + 1], gg[j % 2][:, :], ALU.add, ALU.mult),
                x, m, free_uf[j % 2])
        free_F[2 * (j % 2)] = free_gg[j % 2] = x
        k = FC * g + j
        d = u[k % NU]
        free_uf[j % 2] = uw[k] = split(ph, d[0][:, :], d[1][:, :], uf[j % 2][:, :], ur.get((k - NU) // FC), x)

    def out(g, i):
        t, n = 4 * g + i, 0
        for j in range(FC):
            d = u[(FC * g + j) % NU]
            for x, z in PASSES:
                m = pe(lambda e, j=j, d=d, x=x, z=z, n=n: e.matmul(Y[i % 2][:, 0:D], d[x][:, i * 128:i * 128 + 128], w2[z][:, j, :],
                                                                  start=n == 0, stop=n == 3 * FC - 1), uw[FC * g + j], c_w2, free_Y[i % 2])
                n += 1
        ur[g] = m
        z = free_Y[i % 2] = dve(lambda e: e.tensor_tensor(xs[:, t, :], Y[i % 2][:, 0:D], xs[:, t, :], ALU.add), m, shift_read(shifted, t))
        z = dve(lambda e: e.tensor_tensor(xs[:, t, :], xs[:, t, :], b2[:, :], ALU.add), z, c_r2)
        if last:
            z = pool(lambda e: e.tensor_tensor(xs[:, t, :], xs[:, t, :], xo[g % 2][:, i, :], ALU.add), z, xin[g])
            if i == 3:
                xor_[g] = z
                b, w = divmod(4 * g, W)
                done[g] = sp.dma(cy, lambda e: e.dma_start(y[b, w * 128:w * 128 + 512, :].rearrange("(w p) d -> p w d", p=128),
                                                           xs[:, 4 * g:4 * g + 4, :]), z)

    def fetch(g):
        b, w = divmod(4 * g, W)
        xin[g] = sp.dma(cx[g % 2], lambda e: e.dma_start(xo[g % 2][:, :, :], x1[b, w * 128:w * 128 + 512, :].rearrange("(w p) d -> p w d", p=128)),
                        xor_.get(g - 2))

    for i in range(4):
        statistics(0, i)
    for i in range(4):
        normal(0, i)
        turned(0, i)

    c_w1 = [split(ph, w1[0][:, c, :], w1[1][:, c, :], r1[:, c, :], None, c_r1, scale=lg[:, c:c + 1]) for c in range(2)]
    for j in range(2 * FC):
        for c in range(2):
            m = pe(lambda e, j=j, c=c: e.matmul(F[3][0:FW, j:j + 1], r1[:, c, j * FW:j * FW + FW], lb[:, c:c + 1],
                                                start=c == 0, stop=c == 1, skip_group_check=True), c_r1)
    c_b1 = free_F[3] = dve(lambda e: e.tensor_tensor(b1[:, :], F[3][0:FW, 0:2 * FC], b1[:, :], ALU.add), m)
    c_w2 = None
    for i in range(4):
        statistics(1, i)
    for g in range(NG + 1):
        if last and g < NG:
            fetch(g)
        if g + 3 < NG:
            shifted[g + 3] = shift(ph, xs, sh[g % 3], csh[g % 3], g + 3, sh_read[g])
        for j in range(FC):
            if g + 1 < NG and j < 4:
                normal(g + 1, j)
            if g < NG:
                hidden(g, j)
            if not c_w2:
                c_w2 = split(ph, w2[0][:, :, :], w2[1][:, :, :], r2[:, :, :], None, c_r2)
            if g + 1 < NG and 1 <= j <= 4:
                turned(g + 1, j - 1)
            if g and j in (1, 2):
                out(g - 1, 2 * j - 2)
                out(g - 1, 2 * j - 1)
            if g + 2 < NG and 2 <= j:
                statistics(g + 2, j - 2)
    if last:
        sp(None, done[NG - 1])
    ph.run()


def program(nc, a, y):
    x1 = nc.dram_tensor("x1", [NB, L, D], F32, kind="Internal").ap()
    with nc.sbuf_tensor("xs", [128, NT, D], F32) as xs:
        attention(nc, xs, x1, a)
        for layer in range(2):
            local_layer(nc, xs, layer, a)
            feed_forward(nc, xs, layer, layer == 1, x1, y, a)


def kernel(**inputs):
    import concourse.bacc as bacc
    from concourse.bass_utils import run_bass_kernel_spmd

    i = {k.removeprefix("L0_"): np.asarray(x) for k, x in inputs.items()}
    pad = lambda x, axis: np.concatenate([x, np.zeros([FW * FC - 682 if k == axis else n for k, n in enumerate(x.shape)], x.dtype)], axis)
    halves = lambda x, axis: np.concatenate([pad(h, axis) for h in np.split(x, 2, axis)], axis)
    two = lambda x: np.stack(np.split(x, 2, -1), -1)
    swap = lambda x: np.concatenate([x[:, 32:], x[:, :32]], 1)
    qs, ks = i["ffn_q_scale"], i["ffn_k_scale"]
    arrays = dict(
        x=i["attn_x"], wq=i["attn_Wq"].T, wk=i["attn_Wk"].T, wv=i["attn_Wv"].T, wo=i["attn_Wo"].T,
        bq=two(i["attn_bq"]), bk=two(i["attn_bk"]), bv=i["attn_bv"], bo=i["attn_bo"], lam=i["attn_prior_lambda"].reshape(1),
        prior=prior(), wide=wide_prior(), sel=np.concatenate([np.eye(32, dtype=np.float32)] * 3), ident=np.eye(128, dtype=np.float32),
        wqkv=i["ffn_wqkv"], lwo=i["ffn_wo"], rotary=rotary(), causal=causal(),
        qsc=np.concatenate([qs, swap(qs), ks, swap(ks)], 1),
        w1=halves(i["ffn_w1"], 2), b1=halves(i["ffn_b1"], 1).reshape(2, 2 * FC, FW).transpose(0, 2, 1),
        w2=pad(i["ffn_w2"], 1), b2=i["ffn_b2"], lg=two(i["ffn_ln_g"]), lb=two(i["ffn_ln_b"]))
    nc = bacc.Bacc("TRN2", target_bir_lowering=False, num_devices=1)
    given, a = {}, {}
    for name, x in arrays.items():
        given["in_" + name] = x = np.ascontiguousarray(x)
        a[name] = nc.dram_tensor("in_" + name, x.shape, mybir.dt.from_np(x.dtype), kind="ExternalInput").ap()
    y = nc.dram_tensor("out", (NB, L, D), F32, kind="ExternalOutput").ap()
    program(nc, a, y)
    r = run_bass_kernel_spmd(nc, [given], core_ids=[0])
    return r.results[0]["out"]
```

```python
from contextlib import ExitStack

import numpy as np
import concourse.bass as bass
from concourse import mybir

F32 = mybir.dt.float32
BF16 = mybir.dt.bfloat16
F32R = mybir.dt.float32r
ALU = mybir.AluOpType
ACT = mybir.ActivationFunctionType
X = mybir.AxisListType.X

NB, L, D = 4, 2048, 256
W = L // 128
NT = NB * W
EPS = 1e-5
HA, DA = 16, 16
BAND = 59
WIN = 32 + 2 * BAND
WIDE0 = 512
QPART = [0, 1, 2, 0, 1, 0]
KPART = [0, 0, 0, 1, 1, 2]


class Op:
    def __init__(self, lane, fn, waits, sem=None, val=None):
        self.lane, self.fn, self.waits = lane, fn, waits
        self.sem, self.val, self.signals, self.dma = sem, val, False, sem is not None


def flat(waits):
    out = []
    for w in waits:
        out += flat(w) if isinstance(w, (list, tuple)) else [] if w is None else [w]
    return out


class Lane:

    def __init__(self, sem):
        self.sem, self.ops = sem, []

    def __call__(self, fn, *waits):
        op = Op(self, fn, flat(waits))
        for w in op.waits:
            w.signals = True
        self.ops.append(op)
        return op

    def dma(self, counter, fn, *waits):
        counter.n += 16
        op = Op(self, fn, flat(waits), counter.sem, counter.n)
        for w in op.waits:
            w.signals = True
        self.ops.append(op)
        return op

    def number(self):
        n = 0
        for op in self.ops:
            if op.signals and not op.dma:
                n += 1
                op.sem, op.val = self.sem, n

    def emit(self, eng):
        seen = {}
        for op in self.ops:
            need = {}
            for w in op.waits:
                need[w.sem] = max(need.get(w.sem, 0), w.val)
            for s, v in need.items():
                if seen.get(s, 0) < v:
                    eng.wait_ge(s, v)
                    seen[s] = v
            inst = op.fn and op.fn(eng)
            if op.dma:
                inst.then_inc(op.sem, 16)
            elif op.signals:
                inst.then_inc(op.sem, 1)


class Counter:

    def __init__(self, sem):
        self.sem, self.n = sem, 0


class Phase:

    def __init__(self, nc, tag):
        self.nc, self.tag, self.ctx = nc, tag, ExitStack()
        self.pe, self.act, self.dve, self.pool, self.sp = (Lane(self.sem(n)) for n in ("pe", "act", "dve", "pool", "sp"))

    def sem(self, name):
        return self.ctx.enter_context(self.nc.semaphore(f"{self.tag}_{name}"))

    def counter(self, name):
        return Counter(self.sem(name))

    def sb(self, name, shape, dt=F32):
        return self.ctx.enter_context(self.nc.sbuf_tensor(f"{self.tag}_{name}", shape, dt))

    def ps(self, name, shape, dt=F32):
        return self.ctx.enter_context(self.nc.psum_tensor(f"{self.tag}_{name}", shape, dt))

    def run(self):
        lanes = dict(tensor=self.pe, scalar=self.act, vector=self.dve, gpsimd=self.pool, sync=self.sp)
        for lane in lanes.values():
            lane.number()
        with self.nc.Block() as block:
            for name, lane in lanes.items():
                def body(eng, lane=lane):
                    lane.emit(eng)
                {"tensor": block.tensor, "scalar": block.scalar, "vector": block.vector,
                 "gpsimd": block.gpsimd, "sync": block.sync}[name](body)
        self.ctx.close()


def prior():
    i, c = np.arange(32, dtype=np.float32)[:, None], np.arange(WIN, dtype=np.float32)[None, :]
    delta = np.abs(c - np.float32(BAND) - i)
    g = np.zeros_like(delta)
    for p, w, s in ((1.0, 0.8, 0.5), (30.0, 0.4, 2.0)):
        g = g + np.float32(w) * np.exp(-(delta - np.float32(p)) ** 2 / np.float32(2.0 * s * s))
    g[delta > BAND] = 0.0
    return np.concatenate([g, g, g]).astype(np.float32)


def wide_prior():
    d = np.arange(512 + WIDE0 + 128) - WIDE0 - np.arange(128)[:, None]
    one = prior()[0]
    g = np.zeros(d.shape, np.float32)
    near = np.abs(d) <= BAND
    g[near] = one[d[near] + BAND]
    return g


def windows(r0):
    a, e = max(r0 - BAND, 0), min(r0 - BAND + WIN, L)
    while a < e:
        z = min(e, (a // 512 + 1) * 512)
        yield a // 512, a % 512, a - (r0 - BAND), z - a
        a = z


def attention(nc, xs, x1, a):
    ph = Phase(nc, "a")
    pe, act, dve, pool, sp = ph.pe, ph.act, ph.dve, ph.pool, ph.sp
    sb = ph.sb
    at = xs[:, (NB - 1) * W:NB * W, :]
    parts = {"q": sb("qs", [128, 3, L], BF16), "k": sb("ks", [128, 3, L], BF16)}
    qp = [sb(f"qp{i}", [128, L], BF16) for i in range(3)]
    kp = [sb(f"kp{i}", [128, L], BF16) for i in range(3)]
    v = [sb(f"v{i}", [128, W, HA, DA + 1]) for i in range(2)]
    NP = 4
    pr = [sb(f"pr{i}", [128, 1024]) for i in range(NP)]
    xc = [sb(f"xc{i}", [128, 4, D]) for i in range(2)]
    hT = [sb(f"hT{i}", [128, 2, 512]) for i in range(2)]
    wt = {n: sb("w" + n, [128, 2, D]) for n in "qkvo"}
    bias = {n: sb("b" + n, [128, 2]) for n in "qk"}
    brow = {n: sb("r" + n, [128, D]) for n in "vo"}
    ident = sb("ident", [128, 128])
    identb = sb("identb", [128, 128], BF16)
    gt = sb("gt", [96, WIN])
    gp = [sb(f"gp{i}", [96, WIN], BF16) for i in range(3)]
    mt = sb("mt", [96, WIN], BF16)
    gw = sb("gw", [128, 512 + WIDE0 + 128])
    tmp = [sb(f"tmp{i}", [128, 512]) for i in range(2)]
    g1, g2 = tmp[0][0:96, 0:WIN], tmp[1][0:96, 0:WIN]
    osb = sb("osb", [128, 512])
    junk = sb("junk", [128, 512], BF16)
    sel = sb("sel", [96, 32], BF16)
    self32 = sb("self32", [96, 32])
    lam, lam4 = sb("lam", [128, 1]), sb("lam4", [128, 1])
    nh = sb("nh", [128, 4])
    st = sb("st", [128, 4, 6])
    mv, mv2 = sb("mv", [128, W, 2]), sb("mv2", [128, 4, 2])
    rs, rs2 = sb("rs", [128, W]), sb("rs2", [128, 4])
    ve = sb("ve", [128, 4])
    mx = [sb(f"mx{i}", [128, W, 4]) for i in range(2)]
    nm, r1 = sb("nm", [128, W]), sb("r1", [128, W])
    pk = sb("pk", [128, 3, W], BF16)
    row = sb("row", [48, 128], BF16)
    rc = sb("rc", [128, 4, 4])
    bank = [ph.ps(f"b{i}", [128, 512]) for i in range(3)]
    wide = [ph.ps(f"w{i}", [128, 1024]) for i in range(2)]
    po = ph.ps("po", [128, 512])

    cw = ph.counter("cw")
    cl, cs = [ph.counter(f"x{i}") for i in range(2)], [ph.counter(f"res{i}") for i in range(2)]
    chunks = []
    for b in range(NB):
        if b == 0:
            chunks += [(0, "v", j) for j in range(4)]
        if b:
            chunks += [(b - 1, "o", j) for j in range(4)]
        chunks += [(b, 1, j) for j in range(4)]
        if b + 1 < NB:
            chunks += [(b + 1, "v", j) for j in range(4)] + [(b + 1, 0, j) for j in range(4)]
    chunks += [(NB - 1, "o", j) for j in range(4)]
    where = {c: k for k, c in enumerate(chunks)}
    loaded, released = {}, {}

    def load(k):
        if k < len(chunks):
            b, _, j = chunks[k]
            loaded[k] = sp.dma(cl[k % 2], lambda e: e.dma_start(
                xc[k % 2][:, :, :], a["x"][b, j * 512:j * 512 + 512, :].rearrange("(w p) d -> p w d", p=128)), released.get(k - 2))

    load(0)
    load(1)
    for n in "vqko":
        sp.dma(cw, lambda e, n=n: e.dma_start(wt[n][:, :, :], a["w" + n].rearrange("(c p) n -> p c n", p=128)))
    for n in "qk":
        sp.dma(cw, lambda e, n=n: e.dma_start(bias[n][:, :], a["b" + n]))
    for n in "vo":
        sp.dma(cw, lambda e, n=n: e.dma_start(brow[n][:, :], a["b" + n].partition_broadcast(128)))
    sp.dma(cw, lambda e: e.dma_start(lam[:, :], a["lam"].partition_broadcast(128)))
    sp.dma(cw, lambda e: e.dma_start(gt[:, :], a["prior"]))
    sp.dma(cw, lambda e: e.dma_start(self32[:, :], a["sel"]))
    sp.dma(cw, lambda e: e.dma_start(gw[:, :], a["wide"]))
    const = sp.dma(cw, lambda e: e.dma_start(ident[:, :], a["ident"]))

    c_nh = pool(lambda e: e.memset(nh[:, :], -0.5))
    for i in range(3):
        c_one = dve(lambda e, i=i: e.memset(kp[i][96:99, :], 1.0))
    for i in range(2):
        c_v1 = pool(lambda e, i=i: e.memset(v[i][:, :, :, DA:DA + 1], 1.0))
    c_po = dve(lambda e: e.memset(po[:, :], 0.0))

    def constants():
        nonlocal idb, c_sel, c_gw, c_mt
        idb = dve(lambda e: e.tensor_copy(identb[:, :], ident[:, :]), const)
        c_sel = dve(lambda e: e.tensor_copy(sel[:, :], self32[:, :]), const)
        t = dve(lambda e: e.tensor_scalar(lam4[:, :], lam[:, :], 4.0, None, ALU.mult), const)
        c_gw = dve(lambda e: e.tensor_scalar(gw[:, :], gw[:, :], lam4[:, :], None, ALU.mult), t)
        t = dve(lambda e: e.tensor_scalar(gt[:, :], gt[:, :], lam4[0:96, :], None, ALU.mult), t)
        t = dve(lambda e: e.tensor_copy(gp[0][:, :], gt[:, :]), t)
        t = dve(lambda e: e.tensor_tensor(g1, gt[:, :], gp[0][:, :], ALU.subtract), t, free_tmp[0])
        t = dve(lambda e: e.tensor_copy(gp[1][:, :], g1), t)
        t = dve(lambda e: e.tensor_tensor(g2, g1, gp[1][:, :], ALU.subtract), t, free_tmp[1])
        t = dve(lambda e: e.tensor_copy(gp[2][:, :], g2), t)
        free_tmp[0] = free_tmp[1] = t
        for i in range(3):
            c_mt = dve(lambda e, i=i: e.tensor_copy(mt[32 * i:32 * i + 32, :], gp[i][32 * i:32 * i + 32, :]), t)

    idb = c_sel = c_gw = c_mt = None
    banks = [x[:, :] for x in bank] + [wide[i][:, c:c + 512] for i in range(2) for c in (0, 512)]
    freed = [None] * 7
    HELD = object()
    n_banks, turn = 7, 0

    def slot():
        nonlocal turn
        turn += 1
        while freed[turn % n_banks] is HELD:
            turn += 1
        i = turn % n_banks
        was, freed[i] = freed[i], HELD
        return i, banks[i], was

    cp = [ph.counter(f"pack{i}") for i in range(3)]
    cr = [ph.counter(f"row{i}") for i in range(3)]
    pack_of, row_of, qk_read = {}, {}, {}
    free_wide = [None] * 2
    free_pr, free_tmp, free_mx, free_hT = [None] * NP, [None] * 2, [None] * 2, [None] * 2
    free_po, free_osb, free_row, free_pk = c_po, None, None, None
    pk_done, osb_done, norm_last, at_read, junk_w, n_tmp, n_hT, mv2_read, mv_read = None, None, None, None, None, 0, 0, None, None
    pv_last, v_done, pack_last, part_done, mean, normed, hTw, aTw, x1_done = {}, {}, None, {}, {}, {}, {}, {}, {}

    def stats(b, j):
        k = where[b, "v", j]
        for i in range(4):
            t = dve(lambda e, i=i: e.bn_stats(st[:, i, :], xc[k % 2][:, i, :]), loaded[k])
        for i in range(4):
            t = dve(lambda e, i=i: e.bn_aggr(mv[:, 4 * j + i, :], st[:, i, :]), t, mv_read)
        t = dve(lambda e: e.tensor_scalar(ve[:, :], mv[:, 4 * j:4 * j + 4, 1], EPS, None, ALU.add), t)
        mean[b, j] = pool(lambda e: e.tensor_tensor(rs[:, 4 * j:4 * j + 4], ve[:, :], nh[:, :], ALU.pow), t, c_nh)

    def normal(b, kind, j, half):
        nonlocal mv_read
        k = where[b, kind, j]
        for i in (2 * half, 2 * half + 1):
            w = 4 * j + i
            normed[b, kind, j, half] = mv_read = dve(lambda e, i=i, w=w: e.tensor_scalar(
                xc[k % 2][:, i, :], xc[k % 2][:, i, :], mv[:, w, 0:1], rs[:, w:w + 1], ALU.subtract, ALU.mult), mean[b, j], loaded[k])

    def turned(b, kind, j, half):
        nonlocal n_hT
        k = where[b, kind, j]
        if half == 0:
            n_hT += 1
        dst = hT[n_hT % 2]
        s, bk, was = slot()
        for i in (2 * half, 2 * half + 1):
            for c in range(2):
                m = pe(lambda e, i=i, c=c: e.transpose(bk[:, c * 256 + (i % 2) * 128:c * 256 + (i % 2) * 128 + 128],
                                                       xc[k % 2][:, i, c * 128:c * 128 + 128], ident[:, :]),
                       normed[b, kind, j, half], was, const)
        released[k] = m
        hTw[b, kind, j] = freed[s] = act(lambda e: e.activation(dst[:, :, half * 256:half * 256 + 256],
                                                               bk.rearrange("p (c n) -> p c n", c=2), ACT.Copy), m, free_hT[n_hT % 2])
        if half == 1:
            load(k + 2)

    def project(b, c, j, n):
        nonlocal n_tmp
        src, q = hT[n_hT % 2], n_hT % 2
        s, bk, was = slot()
        for cc in range(2):
            m = pe(lambda e, cc=cc: e.matmul(bk, wt[n][:, cc, c * 128:c * 128 + 128], src[:, cc, :], start=cc == 0, stop=cc == 1),
                   hTw[b, c, j], was)
        free_hT[q] = m
        d = [parts[n][:, p, j * 512:j * 512 + 512] for p in range(3)]
        i = n_tmp % 2
        tm = tmp[i][:, :]
        n_tmp += 1
        h0 = act(lambda e: e.activation(d[0], bk, ACT.Identity, bias=bias[n][:, c:c + 1]), m, pack_last)

        def rest():
            r = freed[s] = dve(lambda e: e.scalar_tensor_tensor(tm, bk, bias[n][:, c:c + 1], d[0], ALU.add, ALU.subtract), h0, free_tmp[i])
            h1 = act(lambda e: e.activation(d[1], tm, ACT.Copy), r, pack_last)
            free_tmp[i] = part_done[b, c] = pool(lambda e: e.tensor_tensor(d[2], tm, d[1], ALU.subtract), h1, pack_last)
        return rest

    def values(b, j, half):
        src, q = hT[n_hT % 2], n_hT % 2
        s, bk, was = slot()
        for i in range(2):
            for cc in range(2):
                m = pe(lambda e, cc=cc, i=i: e.matmul(bk[:, i * D:i * D + D], src[:, cc, (2 * half + i) * 128:(2 * half + i) * 128 + 128],
                                                      wt["v"][:, cc, :], start=cc == 0, stop=cc == 1), hTw[b, "v", j], was)
        free_hT[q] = m

        def rest():
            for i in range(2):
                t = dve(lambda e, i=i: e.tensor_tensor(
                    v[b % 2][:, 4 * j + 2 * half + i, :, 0:DA], bk[:, i * D:i * D + D].rearrange("p (h d) -> p h d", d=DA),
                    brow["v"][:, :].rearrange("p (h d) -> p h d", d=DA), ALU.add), m, pv_last.get(b - 2))
            freed[s] = v_done[b] = t
        return rest

    def out_T(b, w0):
        nonlocal n_hT, at_read
        n_hT += w0 % 4 == 0
        dst = hT[n_hT % 2]
        s, bk, was = slot()
        for i in range(2):
            for c in range(2):
                m = pe(lambda e, i=i, c=c: e.transpose(bk[:, c * 256 + i * 128:c * 256 + i * 128 + 128], at[:, w0 + i, c * 128:c * 128 + 128],
                                                       ident[:, :]), norm_last, was)
        at_read = m
        o = (w0 % 4) * 128
        aTw[b, w0] = freed[s] = act(lambda e: e.activation(dst[:, :, o:o + 256], bk.rearrange("p (c n) -> p c n", c=2), ACT.Copy),
                                    m, free_hT[n_hT % 2])

    def out_project(b, w0):
        q = n_hT % 2
        src = hT[q]
        s, bk, was = slot()
        for i in range(2):
            for c in range(2):
                o = ((w0 + i) % 4) * 128
                m = pe(lambda e, i=i, c=c, o=o: e.matmul(bk[:, i * D:i * D + D], src[:, c, o:o + 128], wt["o"][:, c, :],
                                                         start=c == 0, stop=c == 1), aTw[b, w0], was)
        free_hT[q] = m
        k = where[b, "o", w0 // 4]
        i0 = w0 % 4
        x2 = xc[k % 2][:, i0:i0 + 2, :]

        def rest():
            t = freed[s] = dve(lambda e: e.tensor_tensor(x2, bk.rearrange("p (w d) -> p w d", d=D), x2, ALU.add), m, loaded[k])
            t = x1s = dve(lambda e: e.tensor_tensor(x2, x2, brow["o"][:, :].unsqueeze(1).to_broadcast([128, 2, D]), ALU.add), t)
            for i in range(2):
                t = dve(lambda e, i=i: e.bn_stats(st[:, i, :], xc[k % 2][:, i0 + i, :]), x1s)
            for i in range(2):
                t = dve(lambda e, i=i: e.bn_aggr(mv2[:, i0 + i, :], st[:, i, :]), t, mv2_read)
            t = dve(lambda e: e.tensor_scalar(ve[:, 0:2], mv2[:, i0:i0 + 2, 1], EPS, None, ALU.add), t)
            t = pool(lambda e: e.tensor_tensor(rs2[:, i0:i0 + 2], ve[:, 0:2], nh[:, 0:2], ALU.pow), t, c_nh)
            if i0 == 2:
                x1_done[b] = sp.dma(cs[k % 2], lambda e: e.dma_start(
                    x1[b, (w0 - 2) * 128:(w0 + 2) * 128, :].rearrange("(w p) d -> p w d", p=128), xc[k % 2][:, :, :]), x1s)
            seconds.append((b, w0, k, i0, t))
        return rest

    def second():
        nonlocal mv2_read
        if seconds:
            b, w0, k, i0, t = seconds.pop()
            for i in range(2):
                mv2_read = dve(lambda e, i=i: e.tensor_scalar(xs[:, b * W + w0 + i, :], xc[k % 2][:, i0 + i, :], mv2[:, i0 + i, 0:1],
                                                              rs2[:, i0 + i:i0 + i + 1], ALU.subtract, ALU.mult), t, at_read)
            if i0 == 2:
                released[k] = [x1_done[b], mv2_read]
                load(k + 2)

    def pack(g):
        nonlocal pack_last
        b, h = divmod(g, HA)
        s, r0 = g % 3, 16 * (h % 8)
        for n, dst, order in (("q", qp[s], QPART), ("k", kp[s], KPART)):
            for j, p in enumerate(order):
                pack_last = pack_of[g] = sp.dma(cp[s], lambda e, n=n, dst=dst, j=j, p=p: e.dma_start(
                    dst[16 * j:16 * j + 16, :], parts[n][r0:r0 + 16, p, :]), part_done[b, h // 8], qk_read.get(s))

    p1_last = {}

    def pass1(g, qb, c):
        nonlocal junk_w
        s = g % 3
        i, bk, was = slot()
        m = pe(lambda e: e.matmul(bk, qp[s][0:96, qb * 128:qb * 128 + 128], kp[s][0:96, c * 512:c * 512 + 512],
                                  start=True, stop=True), pack_of[g], was)
        o = 512 * c - 128 * qb
        if -512 - BAND < o < 128 + BAND:
            r = junk_w = dve(lambda e: e.tensor_tensor_reduce(junk[:, :], bk, gw[:, o + WIDE0:o + WIDE0 + 512], 1.0, 0.0,
                                                              ALU.add, ALU.max, mx[g % 2][:, qb, c:c + 1]),
                             m, c_gw, free_mx[g % 2], junk_w)
        else:
            r = dve(lambda e: e.tensor_reduce(mx[g % 2][:, qb, c:c + 1], bk, X, ALU.max), m, free_mx[g % 2])
        freed[i] = p1_last[g] = r

    def rows(g):
        nonlocal pk_done
        t = free_mx[g % 2] = dve(lambda e: e.tensor_reduce(nm[:, :], mx[g % 2][:, :, :], X, ALU.max, negate=True), p1_last[g])
        t = dve(lambda e: e.tensor_copy(pk[:, 0, :], nm[:, :]), t, free_pk)
        t = dve(lambda e: e.tensor_tensor(r1[:, :], nm[:, :], pk[:, 0, :], ALU.subtract), t)
        t = dve(lambda e: e.tensor_copy(pk[:, 1, :], r1[:, :]), t)
        pk_done = dve(lambda e: e.tensor_tensor(pk[:, 2, :], r1[:, :], pk[:, 1, :], ALU.subtract), t)

    def rows_T(g):
        nonlocal free_row, free_pk
        s = g % 3
        i, bk, was = slot()
        ptb = bk.bitcast(BF16)
        t = free_pk = pe(lambda e: e.transpose(ptb[0:48, 0:128], pk[:, :, :].rearrange("p a b -> p (a b)"), identb[:, :]), pk_done, idb, was)
        t = freed[i] = dve(lambda e: e.tensor_copy(row[:, :], ptb[0:48, 0:128]), t, free_row)
        for p in range(3):
            free_row = row_of[g] = sp.dma(cr[s], lambda e, p=p: e.dma_start(qp[s][96 + p:97 + p, :], row[16 * p:16 * p + 16, :]),
                                          t, qk_read.get(s))

    exps = {}

    def pass2(g, kb, u):
        s = g % 3
        n = (g * W + kb) * 2 + u
        for c in range(2):
            m = pe(lambda e, c=c: e.matmul(wide[u][:, c * 512:c * 512 + 512], kp[s][0:99, kb * 128:kb * 128 + 128],
                                           qp[s][0:99, u * 1024 + c * 512:u * 1024 + c * 512 + 512],
                                           start=True, stop=True, skip_group_check=True), pack_of[g], row_of[g], c_one, free_wide[u])
        qk_read[s] = m
        for q in range(4):
            for bk, c0, p0, n_ in windows(kb * 128 + 32 * q):
                if bk // 2 == u:
                    o = wide[u][:, bk % 2 * 512:bk % 2 * 512 + 512]
                    m = pe(lambda e, q=q, c0=c0, p0=p0, n_=n_, o=o: e.matmul(
                        o[32 * q:32 * q + 32, c0:c0 + n_], sel[:, :], mt[:, p0:p0 + n_], start=False, stop=True, skip_group_check=True),
                        c_mt, c_sel)
        free_wide[u] = exps[n] = act(lambda e: e.activation(pr[n % NP][:, :], wide[u][:, :], ACT.Exp, scale=0.25), m, free_pr[n % NP])

    def pv(g, kb, js):
        b, h = divmod(g, HA)
        n = (g * W + kb) * 2
        for j in js:
            i = (n + j // 2) % NP
            m = free_pr[i] = pe(lambda e, j=j, i=i: e.matmul(
                po[32 * j:32 * j + DA + 1, :], v[b % 2][:, kb, h, :], pr[i][:, (j % 2) * 512:(j % 2) * 512 + 512],
                start=kb == 0, stop=kb == W - 1, skip_group_check=True),
                exps[n + j // 2], free_po if kb == 0 else None, v_done[b], c_v1)
        pv_last[b] = m

    def finish(g):
        nonlocal free_po, osb_done
        osb_done = free_po = act(lambda e: e.activation(osb[:, :], po[:, :], ACT.Copy), pv_last[g // HA], free_osb)

    def finish_T(g):
        nonlocal free_osb, norm_last
        h = g % HA
        i, bk, was = slot()
        for s in range(4):
            t = free_osb = pe(lambda e, s=s: e.transpose(bk[:, s * 128:s * 128 + 128], osb[:, s * 128:s * 128 + 128], ident[:, :]),
                              osb_done, was)
        z = bk.rearrange("p (s j e) -> p s j e", s=4, j=4)
        r = dve(lambda e: e.reciprocal(rc[:, :, :], z[:, :, :, DA]), t, norm_last)
        norm_last = freed[i] = dve(lambda e: e.tensor_tensor(
            at[:, :, h * DA:h * DA + DA].rearrange("p (j s) d -> p s j d", s=4), z[:, :, :, 0:DA],
            rc[:, :, :].unsqueeze(3).to_broadcast([128, 4, 4, DA]), ALU.mult), r, at_read)

    stats(0, 0)
    for half in range(2):
        normal(0, "v", 0, half)
    for j in range(4):
        for half in range(2):
            turned(0, "v", j, half)
        hTw[0, 0, j] = hTw[0, "v", j]
        rests = [values(0, j, half) for half in range(2)] + [project(0, 0, j, n) for n in "qk"]
        if j < 3:
            stats(0, j + 1)
        for r in rests[:2]:
            r()
        if j == 1:
            constants()
        if j < 3:
            for half in range(2):
                normal(0, "v", j + 1, half)
        for r in rests[2:]:
            r()
    pack(0)
    pack(1)

    LEAD = W + 3

    units, before = {}, {}

    def plan(n, f, *args):
        while n in units:
            n += 1
        units[n] = lambda: f(*args)
        if f is turned:
            before[n - 1] = lambda: normal(*args)
        return n

    S = HA * W
    for b in range(NB):
        n0 = b * S
        if b:
            n = n0 + 2
            for w0 in range(0, W, 2):
                n = plan(n, out_T, b - 1, w0)
                n = plan(n, out_project, b - 1, w0)
        n = n0 + 85
        for j in range(4):
            for f in ((turned, b, 1, j, 0), (turned, b, 1, j, 1), (project, b, 1, j, "q"), (project, b, 1, j, "k")):
                n = plan(n, *f)
        assert n <= n0 + 101
        if b + 1 < NB:
            n = n0 + 114
            for j in range(4):
                n = plan(n, stats, b + 1, j) + 2
                for f in ((turned, b + 1, "v", j, 0), (turned, b + 1, "v", j, 1), (values, b + 1, j, 0), (values, b + 1, j, 1)):
                    n = plan(n + 1, *f)
            n = n0 + 213
            for j in range(4):
                for f in ((turned, b + 1, 0, j, 0), (turned, b + 1, 0, j, 1), (project, b + 1, 0, j, "q"), (project, b + 1, 0, j, "k")):
                    n = plan(n, *f)
            assert n <= n0 + 229
    packs = {16 * (g - 2) + (7 if g % 8 == 0 else 1): g for g in range(2, NB * HA)}

    free_wide[0], free_wide[1] = freed[3:5], freed[5:7]
    n_banks = 3
    after, seconds = [], []
    later = []
    i1 = 0

    def p1_unit(c):
        nonlocal i1
        if i1 < NB * S:
            g, qb = divmod(i1, W)
            pass1(g, qb, c)
            if c == 3:
                i1 += 1
                if qb == W - 1:
                    rows(g)
                    later.append(lambda: rows_T(g))

    for n in range(-LEAD, NB * S + 1):
        if n in packs:
            pack(packs[n])
        todo = list(later)
        later.clear()
        g, kb = divmod(n, W)
        p1_unit(0)
        if 0 <= n < NB * S:
            pass2(g, kb, 0)
        p1_unit(1)
        second()
        if after:
            after.pop()()
        if n in before:
            before[n]()
        if 0 <= n < NB * S:
            pass2(g, kb, 1)
        p1_unit(2)
        if n in units and (rest := units[n]()):
            after.append(rest)
        if n > 0:
            pv(*divmod(n - 1, W), (2,3))
        p1_unit(3)
        if n > 0:
            pv(*divmod(n - 1, W), (0,1))
        if n > 0 and kb == 0:
            finish(g - 1)
            later.append(lambda g=g: finish_T(g - 1))
        for f in todo:
            f()
    for f in later:
        f()

    freed[3:] = [free_wide[0], free_wide[0], free_wide[1], free_wide[1]]
    n_banks = 7
    for w0 in range(0, W, 2):
        out_T(NB - 1, w0)
        second()
        out_project(NB - 1, w0)()
    second()
    sp(None, list(x1_done.values()))
    ph.run()


HL, DL = 8, 64
NEG = -3.3895313892515355e38
FC, FW = 6, 114
ROUNDS = [(0, 112), (112, 15)]


def split(ph, hi, lo, x, free=(), *waits, scale=None):
    if scale is None:
        h = ph.act(lambda e: e.activation(hi, x, ACT.Copy), free, *waits)
        return ph.dve(lambda e: e.tensor_tensor(lo, x, hi.bitcast(F32), ALU.subtract), h, free, *waits)
    h = ph.act(lambda e: e.activation(hi, x, ACT.Copy, scale=scale), free, *waits)
    return ph.dve(lambda e: e.scalar_tensor_tensor(lo, x, scale, hi.bitcast(F32), ALU.mult, ALU.subtract), h, free, *waits)


PASSES = ((0, 0), (0, 1), (1, 0))


def shift(ph, xs, dst, counter, g, waits):
    t = 4 * g
    up, z = xs[:, t:t + 4, 128:256], None
    for p, n in ROUNDS:
        ph.sp.dma(counter, lambda e, p=p, n=n: e.dma_start(dst[p + 1:p + 1 + n, :, :], up[p:p + n, :, :]), waits)
    first = t % W == 0
    if first:
        z = ph.pool(lambda e: e.memset(dst[0:1, 0, :], 0.0), waits)
    o = int(first)
    return [z, ph.sp.dma(counter, lambda e: e.dma_start(dst[0:1, o:4, :], xs[127:128, t - 1 + o:t + 3, 128:256]), waits)]


def shift_read(shifted, t):
    return [shifted[t // 4], shifted[(t + 1) // 4] if (t + 1) % W else None]


def rotary():
    half = np.arange(0, DL, 2, dtype=np.float32)
    inv = np.float32(1.0) / np.float32(10000.0) ** (half / np.float32(DL))
    t = np.arange(L, dtype=np.float32)
    f = t[:, None] * inv[None, :]
    f = np.concatenate([f, f], 1)
    base = (half + np.float32(0.4 * DL)) / np.float32(1.4 * DL)
    power = (t - np.float32(L // 2)) / np.float32(64.0)
    s = base[None, :] ** power[:, None]
    s = np.concatenate([s, s], 1)
    sign = np.concatenate([-np.ones(32), np.ones(32)]).astype(np.float32)
    cos, sin = np.cos(f), np.sin(f) * sign
    e = np.float32(8.0)
    q, k = np.stack([cos * s * e, sin * s * e], 1), np.stack([cos / s, sin / s], 1)
    return np.ascontiguousarray(np.stack([q, k], 1).astype(np.float32).reshape(W, 128, 2, 2, DL).transpose(1, 0, 2, 3, 4))


def causal():
    r, c = np.arange(128)[:, None], np.arange(128)[None, :]
    m = np.concatenate([np.where(c >= r, 0.0, NEG), np.where(c <= r, 0.0, NEG)], 1)
    return np.concatenate([m, m], 1).astype(np.float32)


def local_layer(nc, xs, layer, a):
    ph = Phase(nc, f"l{layer}")
    pe, act, dve, pool, sp = ph.pe, ph.act, ph.dve, ph.pool, ph.sp
    sb = ph.sb
    wq = [sb(f"wqkv{i}", [128, 2, 3 * HL * DL], F32R) for i in range(2)]
    wo = [sb(f"wo{i}", [128, 4, D], F32R) for i in range(2)]
    tab = [sb(f"tab{i}", [128, 2, 2, DL]) for i in range(3)]
    qsc = sb("qsc", [128, 2, 2, DL])
    ident, identb = sb("ident", [128, 128]), sb("identb", [128, 128], BF16)
    mask = sb("mask", [128, 512], BF16)
    nh = sb("nh", [128, 16])
    sh = [sb(f"sh{i}", [128, 4, 128]) for i in range(2)]
    hT = [[sb(f"hT{i}{k}", [128, 256], F32R) for k in range(2)] for i in range(2)]
    qk = sb("qk", [128, 2, HL, DL])
    sq = sb("sq", [128, 2, HL, DL])
    t1 = [sb(f"t1{i}", [128, 2, HL, DL]) for i in range(2)]
    t2 = sb("t2", [128, 2, HL, DL])
    ss, ri = [sb(f"ss{i}", [128, 16]) for i in range(2)], [sb(f"ri{i}", [128, 16]) for i in range(2)]
    qT = [[sb(f"qT{i}{k}", [128, 512], F32R) for k in range(2)] for i in range(2)]
    kT = [[sb(f"kT{i}{k}", [128, 4, 2, 128], F32R) for k in range(2)] for i in range(3)]
    v = [sb(f"v{i}", [128, HL * DL]) for i in range(5)]
    p = [sb(f"p{i}", [128, HL, 2, 128]) for i in range(2)]
    nm, sm, rc = ([sb(f"{n}{i}", [128, HL]) for i in range(2)] for n in ("nm", "sm", "rc"))
    pT = [sb(f"pT{i}", [128, 2, 2, 128]) for i in range(4)]
    oT = [[sb(f"oT{i}{k}", [128, 512], F32R) for k in range(2)] for i in range(2)]
    G = [ph.ps(f"G{i}", [128, 512]) for i in range(2)]
    T = ph.ps("T", [128, 512])
    S = [ph.ps(f"S{i}", [128, 512]) for i in range(2)]
    R = [ph.ps(f"R{i}", [128, 512]) for i in range(2)]
    O = ph.ps("O", [128, 512])

    ci, cq, cw = ph.counter("ci"), [ph.counter(f"cq{i}") for i in range(2)], ph.counter("cw")
    c_ident = sp.dma(ci, lambda e: e.dma_start(ident[:, :], a["ident"]))
    csh = [ph.counter(f"sh{i}") for i in range(2)]
    shifted, sh_read = {}, {}
    shifted[0] = shift(ph, xs, sh[0], csh[0], 0, None)
    stage, c_wq = [x[:, :, :, :].rearrange("p a h d -> p a (h d)") for x in (t1[0], t2)], {}

    def load_wqkv(n, *waits):
        return sp.dma(cq[n % 2], lambda e: e.dma_start(stage[n % 2], a["wqkv"][layer, :, n * 512:n * 512 + 512].rearrange("(c p) n -> p c n", p=128)),
                      *waits)

    c_raw = [load_wqkv(n) for n in range(2)]

    def split_wqkv():
        for n in range(3):
            if n == 2:
                c_raw.append(load_wqkv(2, c_wq[0]))
            c_wq[n] = split(ph, wq[0][:, :, n * 512:n * 512 + 512], wq[1][:, :, n * 512:n * 512 + 512], stage[n % 2], None, c_raw[n])

    ct, tab_of = [ph.counter(f"tab{i}") for i in range(3)], {}

    def load_table(t):
        tab_of[t] = sp.dma(ct[t % 3], lambda e: e.dma_start(tab[t % 3][:, :, :, :], a["rotary"][:, t % W, :, :, :]), tabr.get(t - 3))

    def scale_table(t):
        tab_of[t] = pool(lambda e: e.tensor_tensor(tab[t % 3][:, :, :, :], tab[t % 3][:, :, :, :], qsc[:, :, :, :], ALU.mult), tab_of[t], const)

    tabr = {}
    load_table(0)
    load_table(1)
    sp.dma(cw, lambda e: e.dma_start(qsc[:, :, :, :].rearrange("p a b d -> p (a b d)"), a["qsc"][layer].partition_broadcast(128)))
    mask32, wraw = sq[:, 0, :, :].rearrange("p h d -> p (h d)"), t1[1][:, :, :, :].rearrange("p a h d -> p (a h d)")
    sp.dma(cw, lambda e: e.dma_start(mask32, a["causal"]))
    const = sp.dma(cw, lambda e: e.dma_start(wraw.rearrange("p (c n) -> p c n", n=D), a["lwo"][layer].rearrange("(c p) n -> p c n", p=128)))
    c_nh = pool(lambda e: e.memset(nh[:, :], -0.5))
    idb = dve(lambda e: e.tensor_copy(identb[:, :], ident[:, :]), c_ident)

    def late():
        nonlocal c_mask, c_wo
        c_mask = dve(lambda e: e.tensor_copy(mask[:, :], mask32), const)
        wide = [x[:, :, :].rearrange("p a n -> p (a n)") for x in wo]
        c_wo = split(ph, wide[0], wide[1], wraw, None, const)

    def zero_kT():
        nonlocal c_kT
        c_kT = [dve(lambda e, x=x: e.tensor_scalar(x[:, :, :, :].rearrange("p a h n -> p (a h) n"),
                                                   ident[:, :].unsqueeze(1).to_broadcast([128, 8, 128]), 0.0, None, ALU.mult), c_ident)
                for parts in kT for x in parts]

    c_mask = c_wo = c_kT = None
    free_G, free_T, free_S, free_R, free_O = [None] * 2, [None], [None] * 2, [None] * 2, [None]
    xT, hTr, qkE, qkR, t1w, t1r, ready = {}, {}, {}, {}, {}, {}, {}
    qTw, qTr, kTw, kTr, vw, vr = {}, {}, {}, {}, {}, {}
    pw, pn, pr, recip, pTr, ow, owr, mxs, tsum = {}, {}, {}, {}, {}, {}, {}, {}, {}
    squares, products, inverse, rotated = {}, {}, {}, {}
    t2r, sqr, done = [None], [None], {}

    high = {}

    def low(dst, x, hi, *waits):
        return dve(lambda e: e.tensor_tensor(dst, x, hi.bitcast(F32), ALU.subtract), *waits)

    def x_T(t):
        g = t // 4
        src = [xs[:, t, 0:128], sh[g % 2][:, t % 4, :]]
        for c in range(2):
            m = pe(lambda e, c=c: e.transpose(G[0][:, c * 128:c * 128 + 128], src[c], ident[:, :]), c_ident, shifted[g], free_G[0])
        sh_read[g] = m
        high[t, "x"] = act(lambda e: e.activation(hT[t % 2][0][:, :], G[0][:, 0:256], ACT.Copy), hTr.get(t - 2), m)

    def x_low(t):
        h = hT[t % 2]
        xT[t] = free_G[0] = low(h[1][:, :], G[0][:, 0:256], h[0][:, :], high[t, "x"], hTr.get(t - 2))

    def qkv(t, n):
        g = G[n % 2]
        i = 0
        for x, z in PASSES:
            for c in range(2):
                m = pe(lambda e, c=c, x=x, z=z, i=i: e.matmul(g[:, :], hT[t % 2][x][:, c * 128:c * 128 + 128], wq[z][:, c, n * 512:n * 512 + 512],
                                                              start=i == 0, stop=i == 5), xT[t], c_wq[n], free_G[n % 2])
                i += 1
        hTr[t] = m
        if n < 2:
            free_G[n] = qkE[t, n] = act(lambda e: e.activation(qk[:, n, :, :].rearrange("p h d -> p (h d)"), g[:, :], ACT.Copy),
                                        m, qkR.get(t - 1))
        else:
            free_G[0] = vw[t] = act(lambda e: e.activation(v[t % 5][:, :], g[:, :], ACT.Copy), m, vr.get(t - 5))

    def rotate(t):
        s = t % 2
        src, tb = qk, tab[t % 3]
        squares[t] = act(lambda e: e.activation(sq[:, :, :, :], src[:, :, :, :], ACT.Square),
                         qkE[t, 0], qkE[t, 1], sqr[0], c_mask)
        a1 = dve(lambda e: e.tensor_tensor(t1[s][:, :, :, :], src[:, :, :, :],
                                           tb[:, :, 0, :].unsqueeze(2).to_broadcast([128, 2, HL, DL]), ALU.mult),
                 qkE[t, 0], qkE[t, 1], tab_of[t], c_wo, c_wq[0], t1r.get(t - 2))
        for i in range(2):
            a2 = dve(lambda e, i=i: e.tensor_tensor(
                t2[:, :, :, 32 * i:32 * i + 32], src[:, :, :, 32 - 32 * i:64 - 32 * i],
                tb[:, :, 1, 32 * i:32 * i + 32].unsqueeze(2).to_broadcast([128, 2, HL, 32]), ALU.mult), t2r[0], c_wq[1])
        qkR[t] = [squares[t], a2]
        tabr[t] = a2
        products[t] = [a1, a2]

    def lengths(t):
        s = t % 2
        sqr[0] = r = dve(lambda e: e.tensor_reduce(ss[s][:, :], sq[:, :, :, :].rearrange("p a h d -> p (a h) d"), X, ALU.add),
                         squares[t], t1r.get(t - 2))
        r = dve(lambda e: e.tensor_scalar(ss[s][:, :], ss[s][:, :], 1e-24, None, ALU.max), r)
        r = pool(lambda e: e.tensor_tensor(ri[s][:, :], ss[s][:, :], nh[:, :], ALU.pow), r, c_nh)
        inverse[t] = r
        t2r[0] = rotated[t] = pool(lambda e: e.tensor_tensor(t1[s][:, :, :, :], t1[s][:, :, :, :], t2[:, :, :, :], ALU.add), products[t])

    def scale(t):
        s = t % 2
        flat_ = t1[s][:, :, :, :].rearrange("p a h d -> p (a h) d")
        ready[t] = dve(lambda e: e.tensor_tensor(flat_, flat_, ri[s][:, :].unsqueeze(2).to_broadcast([128, 16, DL]), ALU.mult), rotated[t], inverse[t])

    def qk_T(t, n):
        for i in range(4):
            m = pe(lambda e, i=i: e.transpose(T[:, i * 128:i * 128 + 128],
                                              t1[t % 2][:, n, 2 * i:2 * i + 2, :].rearrange("p h d -> p (h d)"), ident[:, :]),
                   ready[t], free_T[0])
        t1r[t] = m
        if n == 0:
            high[t, n] = act(lambda e: e.activation(qT[t % 2][0][:, :], T[:, :], ACT.Copy), qTr.get(t - 2), m)
        else:
            for i in range(2):
                high[t, n] = act(lambda e, i=i: e.activation(kT[t % 3][0][64 * i:64 * i + 64, :, i, :],
                                                             T[64 * i:64 * i + 64, :].rearrange("p (a n) -> p a n", a=4), ACT.Copy),
                                 kTr.get(t - 3), kTr.get(t - 2), c_kT, m)

    def qk_low(t, n):
        if n == 0:
            q = qT[t % 2]
            free_T[0] = qTw[t] = low(q[1][:, :], T[:, :], q[0][:, :], high[t, n], qTr.get(t - 2))
        else:
            for i in range(2):
                d = [x[64 * i:64 * i + 64, :, i, :] for x in kT[t % 3]]
                free_T[0] = kTw[t] = low(d[1], T[64 * i:64 * i + 64, :].rearrange("p (a n) -> p a n", a=4), d[0],
                                         high[t, n], kTr.get(t - 3), kTr.get(t - 2), c_kT)

    def sim(t, pair):
        w, s = t % W, S[pair % 2]
        z = s[:, :].rearrange("p (h k n) -> p h k n", h=2, k=2)
        pe(lambda e: e.matmul(s[:, :], identb[:, :], mask[:, :], start=True, stop=False, skip_group_check=True),
           idb, c_mask, free_S[pair % 2])
        for k in ([0, 1] if w else [1]):
            for x, y in PASSES:
                m = pe(lambda e, k=k, x=x, y=y: e.matmul(z[:, :, k, :], qT[t % 2][x][:, pair * 128:pair * 128 + 128],
                                                         kT[(t - 1 + k) % 3][y][:, pair, :, :],
                                                         start=False, stop=True, skip_group_check=True), qTw[t], kTw[t])
        qTr[t] = kTr[t] = m
        x = dve(lambda e: e.tensor_reduce(nm[t % 2][:, 2 * pair:2 * pair + 2], s[:, :].rearrange("p (h k) -> p h k", h=2) if w else z[:, :, 1, :],
                                          X, ALU.max, negate=True), m, pw.get((t - 2, pair)))
        for h in range(2):
            hh = 2 * pair + h
            dst = p[t % 2][:, hh, :, :].rearrange("p k n -> p (k n)") if w else p[t % 2][:, hh, 1, :]
            src = s[:, h * 256:h * 256 + 256] if w else z[:, h, 1, :]
            y = act(lambda e, hh=hh, dst=dst, src=src: e.activation(dst, src, ACT.Exp, bias=nm[t % 2][:, hh:hh + 1],
                                                                    accum_out=sm[t % 2][:, hh:hh + 1]),
                    x, pr.get((t - 2, pair)), recip.get((t - 2, pair)))
        free_S[pair % 2] = pw[t, pair] = y

    def normalise(t, pair):
        w, o = t % W, 2 * pair
        recip[t, pair] = r = dve(lambda e: e.reciprocal(rc[t % 2][:, o:o + 2], sm[t % 2][:, o:o + 2]), pw[t, pair], pn.get((t - 2, pair)))
        z = p[t % 2][:, o:o + 2, :, :]
        z = z.rearrange("p h k n -> p h (k n)") if w else z[:, :, 1, :]
        pn[t, pair] = pool(lambda e: e.tensor_tensor(z, z, rc[t % 2][:, o:o + 2].unsqueeze(2).to_broadcast([128, 2, 256 if w else 128]),
                                                     ALU.mult), r)

    def p_T(t, pair):
        w, r = t % W, R[pair % 2]
        ks = [0, 1] if w else [1]
        for h in range(2):
            for k in ks:
                m = pe(lambda e, h=h, k=k: e.transpose(r[:, (2 * k + h) * 128:(2 * k + h) * 128 + 128], p[t % 2][:, 2 * pair + h, k, :], ident[:, :]),
                       pn[t, pair], free_R[pair % 2])
        pr[t, pair] = m
        dst = pT[pair][:, :, :, :].rearrange("p k h n -> p (k h n)")
        lo = 0 if w else 256
        if pair % 2:
            free_R[1] = y = dve(lambda e: e.tensor_copy(dst[:, lo:512], r[:, lo:512]), m, pTr.get(pair))
        else:
            free_R[0] = y = act(lambda e: e.activation(dst[:, lo:512], r[:, lo:512], ACT.Copy), m, pTr.get(pair))
        ks = ks
        pw[t, pair, "T"] = y

    def pv(t, pair):
        w = t % W
        for k in ([0, 1] if w else [1]):
            for h in range(2):
                hh = 2 * pair + h
                m = pe(lambda e, h=h, k=k, hh=hh: e.matmul(
                    O[64 * h:64 * h + 64, pair * 128:pair * 128 + 128], v[(t - 1 + k) % 5][:, hh * DL:hh * DL + DL], pT[pair][:, k, h, :],
                    start=k == 0 or w == 0, stop=k == 1, skip_group_check=True), pw[t, pair, "T"], vw[t], free_O[0])
        pTr[pair] = vr[t - 1] = m
        if pair == 3:
            high[t, "o"] = act(lambda e: e.activation(oT[t % 2][0][:, :], O[:, :], ACT.Copy), owr.get(t - 2), m)

    def o_low(t):
        o = oT[t % 2]
        free_O[0] = ow[t] = low(o[1][:, :], O[:, :], o[0][:, :], high[t, "o"], owr.get(t - 2))

    def out(t):
        i = 0
        for x, z in PASSES:
            for c in range(4):
                m = pe(lambda e, c=c, x=x, z=z, i=i: e.matmul(G[1][:, 0:D], oT[t % 2][x][:, c * 128:c * 128 + 128], wo[z][:, c, :],
                                                              start=i == 0, stop=i == 11), ow[t], c_wo, free_G[1])
                i += 1
        owr[t] = m
        done[t] = free_G[1] = dve(lambda e: e.tensor_tensor(xs[:, t, :], G[1][:, 0:D], xs[:, t, :], ALU.add), m, shift_read(shifted, t))

    def on(f, t, *args):
        if 0 <= t < NT:
            f(t, *args)

    on(x_T, 0)
    on(x_low, 0)
    split_wqkv()
    zero_kT()
    scale_table(0)
    for n in range(NT + 4):
        g = (n + 4) // 4
        if n % 4 == 0 and g < NT // 4:
            shifted[g] = shift(ph, xs, sh[g % 2], csh[g % 2], g, sh_read.get(g - 2))
        if n == 0:
            late()
        if n + 2 < NT:
            load_table(n + 2)
        on(sim, n - 2, 1)
        on(sim, n - 2, 0)
        on(scale, n - 1)
        on(qkv, n, 0)
        on(qkv, n, 1)
        on(rotate, n)
        on(qk_T, n - 1, 0)
        on(qk_low, n - 1, 0)
        on(normalise, n - 2, 0)
        on(qkv, n, 2)
        on(p_T, n - 3, 0)
        on(sim, n - 2, 2)
        on(p_T, n - 3, 1)
        on(scale_table, n + 1)
        on(lengths, n)
        on(pv, n - 3, 0)
        on(normalise, n - 2, 2)
        on(normalise, n - 2, 1)
        on(qk_T, n - 1, 1)
        on(p_T, n - 3, 2)
        on(p_T, n - 3, 3)
        on(pv, n - 3, 1)
        on(sim, n - 2, 3)
        on(x_T, n + 1)
        on(qk_low, n - 1, 1)
        on(pv, n - 3, 2)
        on(out, n - 4)
        on(x_low, n + 1)
        on(pv, n - 3, 3)
        on(normalise, n - 2, 3)
        on(o_low, n - 3)
    ph.run()


def feed_forward(nc, xs, layer, last, x1, y, a):
    ph = Phase(nc, f"f{layer}")
    pe, act, dve, pool, sp = ph.pe, ph.act, ph.dve, ph.pool, ph.sp
    sb = ph.sb
    NG = NT // 4
    w1, w2 = [sb(f"w1{i}", [128, 2, 2 * FC * FW], F32R) for i in range(2)], [sb(f"w2{i}", [FW, FC, D], F32R) for i in range(2)]
    r1, r2 = sb("r1", [128, 2, 2 * FC * FW]), sb("r2", [FW, FC, D])
    b1 = sb("b1", [FW, 2 * FC])
    lg, lb = sb("lg", [128, 2]), sb("lb", [128, 2])
    b2 = sb("b2", [128, D])
    ident = sb("ident", [128, 128])
    nh = sb("nh", [128, 4])
    sh = [sb(f"sh{i}", [128, 4, 128]) for i in range(3)]
    st = sb("st", [128, 2, 6])
    mv, ve, rs = ([sb(f"{n}{i}", [128, 4, w]) for i in range(2)] for n, w in (("mv", 2), ("ve", 1), ("rs", 1)))
    hn = [sb(f"hn{i}", [128, D]) for i in range(4)]
    hT = [[sb(f"hT{i}{k}", [128, 2, 512], F32R) for k in range(2)] for i in range(2)]
    gg = [sb(f"gg{i}", [FW, 512]) for i in range(2)]
    uf = [sb(f"uf{i}", [FW, 512]) for i in range(2)]
    NU = 9
    u = [[sb(f"u{i}_{k}", [FW, 512], F32R) for k in range(2)] for i in range(NU)]
    xo = [sb(f"xo{i}", [128, 4, D]) for i in range(2)] if last else None
    T = [ph.ps(f"T{i}", [128, 512]) for i in range(2)]
    F = [ph.ps(f"F{i}", [128, 512]) for i in range(4)]
    Y = [ph.ps(f"Y{i}", [128, 512]) for i in range(2)]

    c_nh = pool(lambda e: e.memset(nh[:, :], -0.5))
    csh = [ph.counter(f"sh{i}") for i in range(3)]
    cx, cy = [ph.counter(f"x{i}") for i in range(2)], ph.counter("y")
    shifted, sh_read = {}, {}
    shifted[0] = shift(ph, xs, sh[0], csh[0], 0, None)
    cs, c1, cw = ph.counter("cs"), ph.counter("c1"), ph.counter("cw")
    c_ident = sp.dma(cs, lambda e: e.dma_start(ident[:, :], a["ident"]))
    for d, n in ((b1, "b1"), (lg, "lg"), (lb, "lb")):
        sp.dma(c1, lambda e, d=d, n=n: e.dma_start(d[:, :], a[n][layer]))
    c_r1 = sp.dma(c1, lambda e: e.dma_start(r1[:, :, :], a["w1"][layer].rearrange("(c p) n -> p c n", p=128)))
    for g in range(1, min(3, NG)):
        shifted[g] = shift(ph, xs, sh[g], csh[g], g, None)
    sp.dma(cw, lambda e: e.dma_start(b2[:, :], a["b2"][layer].partition_broadcast(128)))
    c_r2 = sp.dma(cw, lambda e: e.dma_start(r2[:, :, :], a["w2"][layer].rearrange("(c p) n -> p c n", p=FW)))

    free_T, free_F, free_Y = [None] * 2, [None] * 4, [None] * 2
    free_hn, hTw, hTr, uw, ur, free_gg, free_uf, stats, normed, mv_read = [None] * 4, {}, {}, {}, {}, [None] * 2, [None] * 2, {}, {}, {}
    xin, xor_, done = {}, {}, {}

    def statistics(g, i):
        s, t = g % 2, 4 * g + i
        prev = mv_read.get(g - 2)
        dve(lambda e: e.bn_stats(st[:, 0, :], xs[:, t, 0:128]), stats.get("st"))
        x = dve(lambda e: e.bn_stats(st[:, 1, :], sh[g % 3][:, i, :]), shifted[g], stats.get("st"))
        x = stats["st"] = dve(lambda e: e.bn_aggr(mv[s][:, i, :], st[:, :, :].rearrange("p a b -> p (a b)")), x, prev)
        if i == 3:
            x = dve(lambda e: e.tensor_scalar(ve[s][:, :, 0], mv[s][:, :, 1], EPS, None, ALU.add), x, stats.get(g - 2))
            stats[g] = pool(lambda e: e.tensor_tensor(rs[s][:, :, 0], ve[s][:, :, 0], nh[:, :], ALU.pow), x, c_nh, prev)

    def normal(g, i):
        s, t = g % 2, 4 * g + i
        for c, src in enumerate((xs[:, t, 0:128], sh[g % 3][:, i, :])):
            n = dve(lambda e, c=c, src=src: e.tensor_scalar(hn[i][:, c * 128:c * 128 + 128], src, mv[s][:, i, 0:1], rs[s][:, i, :],
                                                            ALU.subtract, ALU.mult), stats[g], free_hn[i])
        sh_read[g] = mv_read[g] = normed[g, i] = n

    def turned(g, i):
        for c in range(2):
            m = pe(lambda e, c=c: e.transpose(T[c][:, i * 128:i * 128 + 128], hn[i][:, c * 128:c * 128 + 128], ident[:, :]),
                   normed[g, i], c_ident, free_T[c] if i == 0 else None)
        free_hn[i] = m
        if i == 3:
            for c in range(2):
                free_T[c] = hTw[g] = split(ph, hT[g % 2][0][:, c, :], hT[g % 2][1][:, c, :], T[c][:, :], hTr.get(g - 2), m)

    def hidden(g, j):
        fa, fg = F[2 * (j % 2)], F[2 * (j % 2) + 1]
        for f, k, o in ((fg, FC + j, 1), (fa, j, 0)):
            n = 0
            for x, z in PASSES:
                for c in range(2):
                    m = pe(lambda e, c=c, f=f, k=k, x=x, z=z, n=n: e.matmul(
                        f[0:FW, :], w1[x][:, c, k * FW:k * FW + FW], hT[g % 2][z][:, c, :], start=n == 0, stop=n == 5),
                        hTw[g], c_w1, free_F[2 * (j % 2) + o])
                    n += 1
            if o:
                mg = m
        hTr[g] = m
        x = free_F[2 * (j % 2) + 1] = act(lambda e: e.activation(gg[j % 2][:, :], fg[0:FW, :], ACT.Gelu, bias=b1[:, FC + j:FC + j + 1]),
                                          mg, c_b1, free_gg[j % 2])
        x = dve(lambda e: e.scalar_tensor_tensor(uf[j % 2][:, :], fa[0:FW, :], b1[:, j:j + 1], gg[j % 2][:, :], ALU.add, ALU.mult),
                x, m, free_uf[j % 2])
        free_F[2 * (j % 2)] = free_gg[j % 2] = x
        k = FC * g + j
        d = u[k % NU]
        free_uf[j % 2] = uw[k] = split(ph, d[0][:, :], d[1][:, :], uf[j % 2][:, :], ur.get((k - NU) // FC), x)

    def out(g, i):
        t, n = 4 * g + i, 0
        for j in range(FC):
            d = u[(FC * g + j) % NU]
            for x, z in PASSES:
                m = pe(lambda e, j=j, d=d, x=x, z=z, n=n: e.matmul(Y[i % 2][:, 0:D], d[x][:, i * 128:i * 128 + 128], w2[z][:, j, :],
                                                                  start=n == 0, stop=n == 3 * FC - 1), uw[FC * g + j], c_w2, free_Y[i % 2])
                n += 1
        ur[g] = m
        z = free_Y[i % 2] = dve(lambda e: e.tensor_tensor(xs[:, t, :], Y[i % 2][:, 0:D], xs[:, t, :], ALU.add), m, shift_read(shifted, t))
        z = dve(lambda e: e.tensor_tensor(xs[:, t, :], xs[:, t, :], b2[:, :], ALU.add), z, c_r2)
        if last:
            z = pool(lambda e: e.tensor_tensor(xs[:, t, :], xs[:, t, :], xo[g % 2][:, i, :], ALU.add), z, xin[g])
            if i == 3:
                xor_[g] = z
                b, w = divmod(4 * g, W)
                done[g] = sp.dma(cy, lambda e: e.dma_start(y[b, w * 128:w * 128 + 512, :].rearrange("(w p) d -> p w d", p=128),
                                                           xs[:, 4 * g:4 * g + 4, :]), z)

    def fetch(g):
        b, w = divmod(4 * g, W)
        xin[g] = sp.dma(cx[g % 2], lambda e: e.dma_start(xo[g % 2][:, :, :], x1[b, w * 128:w * 128 + 512, :].rearrange("(w p) d -> p w d", p=128)),
                        xor_.get(g - 2))

    for i in range(4):
        statistics(0, i)
    for i in range(4):
        normal(0, i)
        turned(0, i)

    c_w1 = [split(ph, w1[0][:, c, :], w1[1][:, c, :], r1[:, c, :], None, c_r1, scale=lg[:, c:c + 1]) for c in range(2)]
    for j in range(2 * FC):
        for c in range(2):
            m = pe(lambda e, j=j, c=c: e.matmul(F[3][0:FW, j:j + 1], r1[:, c, j * FW:j * FW + FW], lb[:, c:c + 1],
                                                start=c == 0, stop=c == 1, skip_group_check=True), c_r1)
    c_b1 = free_F[3] = dve(lambda e: e.tensor_tensor(b1[:, :], F[3][0:FW, 0:2 * FC], b1[:, :], ALU.add), m)
    c_w2 = None
    for i in range(4):
        statistics(1, i)
    for g in range(NG + 1):
        if last and g < NG:
            fetch(g)
        if g + 3 < NG:
            shifted[g + 3] = shift(ph, xs, sh[g % 3], csh[g % 3], g + 3, sh_read[g])
        for j in range(FC):
            for i in ((0, 1), (2,), (3,), (), (), ())[j] if g + 1 < NG else ():
                normal(g + 1, i)
            if g < NG:
                hidden(g, j)
            if not c_w2:
                c_w2 = split(ph, w2[0][:, :, :], w2[1][:, :, :], r2[:, :, :], None, c_r2)
            if g and j in (1, 2):
                out(g - 1, 2 * j - 2)
                out(g - 1, 2 * j - 1)
            for i in ((), (0,), (1,), (2, 3), (), ())[j] if g + 1 < NG else ():
                turned(g + 1, i)
            if g + 2 < NG and 2 <= j:
                statistics(g + 2, j - 2)
    if last:
        sp(None, done[NG - 1])
    ph.run()


def program(nc, a, y):
    x1 = nc.dram_tensor("x1", [NB, L, D], F32, kind="Internal").ap()
    with nc.sbuf_tensor("xs", [128, NT, D], F32) as xs:
        attention(nc, xs, x1, a)
        for layer in range(2):
            local_layer(nc, xs, layer, a)
            feed_forward(nc, xs, layer, layer == 1, x1, y, a)


def kernel(**inputs):
    import concourse.bacc as bacc
    from concourse.bass_utils import run_bass_kernel_spmd

    i = {k.removeprefix("L0_"): np.asarray(x) for k, x in inputs.items()}
    pad = lambda x, axis: np.concatenate([x, np.zeros([FW * FC - 682 if k == axis else n for k, n in enumerate(x.shape)], x.dtype)], axis)
    halves = lambda x, axis: np.concatenate([pad(h, axis) for h in np.split(x, 2, axis)], axis)
    two = lambda x: np.stack(np.split(x, 2, -1), -1)
    swap = lambda x: np.concatenate([x[:, 32:], x[:, :32]], 1)
    qs, ks = i["ffn_q_scale"], i["ffn_k_scale"]
    arrays = dict(
        x=i["attn_x"], wq=i["attn_Wq"].T, wk=i["attn_Wk"].T, wv=i["attn_Wv"].T, wo=i["attn_Wo"].T,
        bq=two(i["attn_bq"]), bk=two(i["attn_bk"]), bv=i["attn_bv"], bo=i["attn_bo"], lam=i["attn_prior_lambda"].reshape(1),
        prior=prior(), wide=wide_prior(), sel=np.concatenate([np.eye(32, dtype=np.float32)] * 3), ident=np.eye(128, dtype=np.float32),
        wqkv=i["ffn_wqkv"], lwo=i["ffn_wo"], rotary=rotary(), causal=causal(),
        qsc=np.concatenate([qs, swap(qs), ks, swap(ks)], 1),
        w1=halves(i["ffn_w1"], 2), b1=halves(i["ffn_b1"], 1).reshape(2, 2 * FC, FW).transpose(0, 2, 1),
        w2=pad(i["ffn_w2"], 1), b2=i["ffn_b2"], lg=two(i["ffn_ln_g"]), lb=two(i["ffn_ln_b"]))
    nc = bacc.Bacc("TRN2", target_bir_lowering=False, num_devices=1)
    given, a = {}, {}
    for name, x in arrays.items():
        given["in_" + name] = x = np.ascontiguousarray(x)
        a[name] = nc.dram_tensor("in_" + name, x.shape, mybir.dt.from_np(x.dtype), kind="ExternalInput").ap()
    y = nc.dram_tensor("out", (NB, L, D), F32, kind="ExternalOutput").ap()
    program(nc, a, y)
    r = run_bass_kernel_spmd(nc, [given], core_ids=[0])
    return r.results[0]["out"]
```
